# Optimizing a Trainium2 kernel written in Bass

```python
import numpy as np
import jax
import jax.numpy as jnp

def _softmax(x, axis=-1):
    return jax.nn.softmax(x, axis=axis)

def _gelu(x):
    return jax.nn.gelu(x, approximate=True)

def _silu(x):
    return jax.nn.silu(x)

def _sigmoid(x):
    return jax.nn.sigmoid(x)

def _layernorm(x, axis=-1, eps=1e-05):
    m = jnp.mean(x, axis=axis, keepdims=True)
    v = jnp.var(x, axis=axis, keepdims=True)
    return (x - m) / jnp.sqrt(v + eps)

def _scatter_add(tgt, idx, src, axis=0):
    return tgt.at[idx].add(src)

def _segment_sum(src, seg, n):
    return jax.ops.segment_sum(src, seg, n)
kernel_name = 'mk_gnn_ffn_d2_gnn_r8_86608a'

def setup_inputs(seed: int=0):
    np.random.seed(seed)
    _w = jnp.asarray

    def _rec_inputs():
        import jax
        import jax.numpy as jnp
        _gk = jax.random.key(seed)
        x = -0.0002117 + 1 * jax.random.normal(jax.random.fold_in(_gk, 1), (6250, 256), jnp.float32)
        src = jax.random.randint(jax.random.fold_in(_gk, 2), (200000,), 0, 6250, jnp.int32)
        dst = jax.random.randint(jax.random.fold_in(_gk, 3), (200000,), 0, 6250, jnp.int32)
        _o = jnp.argsort(dst, stable=True)
        src = src[_o]
        dst = dst[_o]
        edge_type_8 = jax.random.randint(jax.random.fold_in(_gk, 13), (200000,), 0, 8, jnp.int32)
        edge_weight = jax.random.uniform(jax.random.fold_in(_gk, 14), (200000,), jnp.float32, 0.0, 1)
        return (x, src, dst, edge_type_8, edge_weight)
    x, src, dst, edge_type_8, edge_weight = _rec_inputs()

    def _L0_gnn_setup():
        import jax, jax.numpy as jnp
        import numpy as np
        N_NODES = 12500
        N_EDGES = 200000
        D_IN = 256
        D_OUT = 256
        key = jax.random.key(seed)
        k1, k2, k3, k4, k5 = jax.random.split(key, 5)
        x = jax.random.normal(k1, (N_NODES, D_IN), dtype=jnp.float32)
        edge_src = jax.random.randint(k2, (N_EDGES,), 0, N_NODES, dtype=jnp.int32)
        edge_dst = jax.random.randint(k3, (N_EDGES,), 0, N_NODES, dtype=jnp.int32)
        edge_val = jax.random.uniform(k4, (N_EDGES,), dtype=jnp.float32)
        stdv = 1.0 / np.sqrt(D_OUT)
        weight = jax.random.uniform(k5, (D_IN, D_OUT), dtype=jnp.float32, minval=-stdv, maxval=stdv)
        return {'x': x, 'edge_src': edge_src, 'edge_dst': edge_dst, 'edge_val': edge_val, 'weight': weight}
    _L0_gnn_all = _L0_gnn_setup()
    _L0_gnn_in = {k: v for k, v in _L0_gnn_all.items() if k in ('weight',)}
    del _L0_gnn_all

    def _L0_ffn_setup():
        import math
        import jax, jax.numpy as jnp
        import numpy as np
        CAPACITY_FACTOR = 1.25
        TOP_K = 2
        LN_EPS = 1e-05

        def _layer_norm(x, gamma, beta):
            mu = jnp.mean(x, axis=-1, keepdims=True)
            var = jnp.var(x, axis=-1, keepdims=True)
            return (x - mu) * jax.lax.rsqrt(var + LN_EPS) * gamma + beta
        key = jax.random.key(seed)
        ks = jax.random.split(key, 4)
        B, S, D, F, E = (8, 512, 256, 512, 8)
        x = jax.random.normal(ks[0], (B, S, D), dtype=jnp.float32)
        Wr = jax.random.normal(ks[1], (D, E), dtype=jnp.float32) / np.sqrt(D)
        br = jnp.zeros((E,), jnp.float32)
        W1 = jax.random.normal(ks[2], (E, D, F), dtype=jnp.float32) / np.sqrt(D)
        b1 = jnp.zeros((E, F), jnp.float32)
        W2 = jax.random.normal(ks[3], (E, F, D), dtype=jnp.float32) / np.sqrt(F)
        b2 = jnp.zeros((E, D), jnp.float32)
        gamma = jnp.ones((D,), jnp.float32)
        beta = jnp.zeros((D,), jnp.float32)
        return {'x': x, 'Wr': Wr, 'br': br, 'W1': W1, 'b1': b1, 'W2': W2, 'b2': b2, 'gamma': gamma, 'beta': beta}
    _L0_ffn_all = _L0_ffn_setup()
    _L0_ffn_in = {k: v for k, v in _L0_ffn_all.items() if k in ('Wr', 'br', 'W1', 'b1', 'W2', 'b2', 'gamma', 'beta')}
    del _L0_ffn_all

    def _L1_gnn_setup():
        import jax, jax.numpy as jnp
        import numpy as np
        N = 3750
        E = 75000
        FIN = 256
        FOUT = 256
        R = 8
        key = jax.random.key(seed)
        ks = jax.random.split(key, 6)
        x = jax.random.normal(ks[0], (N, FIN), dtype=jnp.float32)
        W = jax.random.normal(ks[1], (R, FIN, FOUT), dtype=jnp.float32) * (1.0 / np.sqrt(FIN))
        W_root = jax.random.normal(ks[2], (FIN, FOUT), dtype=jnp.float32) * (1.0 / np.sqrt(FIN))
        bias = jax.random.normal(ks[3], (FOUT,), dtype=jnp.float32) * 0.01
        edge_index = jax.random.randint(ks[4], (2, E), 0, N, dtype=jnp.int64)
        edge_type = jax.random.randint(ks[5], (E,), 0, R, dtype=jnp.int64)
        return {'x': x, 'W': W, 'W_root': W_root, 'bias': bias, 'edge_index': edge_index, 'edge_type': edge_type}
    _L1_gnn_all = _L1_gnn_setup()
    _L1_gnn_in = {k: v for k, v in _L1_gnn_all.items() if k in ('W', 'W_root', 'bias')}
    del _L1_gnn_all

    def _L1_ffn_setup():
        import jax, jax.numpy as jnp
        import numpy as np
        B, T, D, H, E = (16, 512, 256, 512, 8)
        key = jax.random.key(seed)
        ks = jax.random.split(key, 5)
        x = jax.random.normal(ks[0], (B, T, D), dtype=jnp.float32)
        gate_w = jax.random.normal(ks[1], (D, E), dtype=jnp.float32) * 0.02
        gate_b = jnp.zeros((E,), dtype=jnp.float32)
        W1 = jax.random.normal(ks[2], (E, D, H), dtype=jnp.float32) * 0.02
        b1 = jnp.zeros((E, H), dtype=jnp.float32)
        W2 = jax.random.normal(ks[3], (E, H, D), dtype=jnp.float32) * 0.02
        b2 = jnp.zeros((E, D), dtype=jnp.float32)
        return {'x': x, 'gate_w': gate_w, 'gate_b': gate_b, 'W1': W1, 'b1': b1, 'W2': W2, 'b2': b2}
    _L1_ffn_all = _L1_ffn_setup()
    _L1_ffn_in = {k: v for k, v in _L1_ffn_all.items() if k in ('gate_w', 'gate_b', 'W1', 'b1', 'W2', 'b2')}
    del _L1_ffn_all
    return {'x': x, 'src': src, 'dst': dst, 'edge_type_8': edge_type_8, 'edge_weight': edge_weight, 'L0_gnn_weight': _L0_gnn_in['weight'], 'L0_ffn_Wr': _L0_ffn_in['Wr'], 'L0_ffn_br': _L0_ffn_in['br'], 'L0_ffn_W1': _L0_ffn_in['W1'], 'L0_ffn_b1': _L0_ffn_in['b1'], 'L0_ffn_W2': _L0_ffn_in['W2'], 'L0_ffn_b2': _L0_ffn_in['b2'], 'L0_ffn_gamma': _L0_ffn_in['gamma'], 'L0_ffn_beta': _L0_ffn_in['beta'], 'L1_gnn_W': _L1_gnn_in['W'], 'L1_gnn_W_root': _L1_gnn_in['W_root'], 'L1_gnn_bias': _L1_gnn_in['bias'], 'L1_ffn_gate_w': _L1_ffn_in['gate_w'], 'L1_ffn_gate_b': _L1_ffn_in['gate_b'], 'L1_ffn_W1': _L1_ffn_in['W1'], 'L1_ffn_b1': _L1_ffn_in['b1'], 'L1_ffn_W2': _L1_ffn_in['W2'], 'L1_ffn_b2': _L1_ffn_in['b2']}

def reference(x, src, dst, edge_type_8, edge_weight, L0_gnn_weight, L0_ffn_Wr, L0_ffn_br, L0_ffn_W1, L0_ffn_b1, L0_ffn_W2, L0_ffn_b2, L0_ffn_gamma, L0_ffn_beta, L1_gnn_W, L1_gnn_W_root, L1_gnn_bias, L1_ffn_gate_w, L1_ffn_gate_b, L1_ffn_W1, L1_ffn_b1, L1_ffn_W2, L1_ffn_b2):
    import jax
    import jax.numpy as jnp

    def _L0_gnn_ref(x, edge_src, edge_dst, edge_val, weight):
        import jax, jax.numpy as jnp
        import numpy as np
        N_NODES = 12500
        N_EDGES = 200000
        D_IN = 256
        D_OUT = 256
        msgs = x[edge_src] * edge_val[:, None]
        agg = jax.ops.segment_sum(msgs, edge_dst, num_segments=x.shape[0])
        return agg @ weight

    def _L0_ffn_ref(x, Wr, br, W1, b1, W2, b2, gamma, beta):
        import math
        import jax, jax.numpy as jnp
        import numpy as np
        CAPACITY_FACTOR = 1.25
        TOP_K = 2
        LN_EPS = 1e-05

        def _layer_norm(x, gamma, beta):
            mu = jnp.mean(x, axis=-1, keepdims=True)
            var = jnp.var(x, axis=-1, keepdims=True)
            return (x - mu) * jax.lax.rsqrt(var + LN_EPS) * gamma + beta
        B, S, D = x.shape
        E = Wr.shape[1]
        N = B * S
        K = TOP_K
        logits = jnp.mean(x, axis=1) @ Wr + br
        routing_weights = jax.nn.softmax(logits, axis=-1)
        capacity = float(math.ceil(N * CAPACITY_FACTOR / E))
        expected_loads = routing_weights.sum(axis=0) * (N / B)
        scale = jnp.where(expected_loads > capacity, capacity / expected_loads, 1.0)
        routing_weights = jax.nn.softmax(routing_weights * scale, axis=-1)
        rw_tok = jnp.broadcast_to(routing_weights[:, None, :], (B, S, E)).reshape(N, E)
        top_w, top_i = jax.lax.top_k(rw_tok, K)
        top_w = jax.nn.softmax(top_w, axis=-1)
        xf = x.reshape(N, D)
        h = jax.nn.gelu(jnp.einsum('nd,edf->enf', xf, W1) + b1[:, None, :], approximate=False)
        y = jnp.einsum('enf,efd->end', h, W2) + b2[:, None, :]
        w_dense = jnp.zeros((N, E), x.dtype).at[jnp.arange(N)[:, None], top_i].add(top_w)
        out = jnp.einsum('ne,end->nd', w_dense, y).reshape(B, S, D)
        out = _layer_norm(out + x, gamma, beta)
        return out

    def _L1_gnn_ref(x, W, W_root, bias, edge_index, edge_type):
        import jax, jax.numpy as jnp
        import numpy as np
        N = 3750
        E = 75000
        FIN = 256
        FOUT = 256
        R = 8
        n, fin = x.shape
        r = W.shape[0]
        src, dst = (edge_index[0], edge_index[1])
        seg = dst * r + edge_type
        sums = jax.ops.segment_sum(x[src], seg, num_segments=n * r)
        cnt = jax.ops.segment_sum(jnp.ones_like(src, dtype=x.dtype), seg, num_segments=n * r)
        mean = (sums / jnp.maximum(cnt, 1.0)[:, None]).reshape(n, r, fin)
        out = jnp.einsum('nri,rio->no', mean, W) + x @ W_root + bias
        return jax.nn.relu(out)

    def _L1_ffn_ref(x, gate_w, gate_b, W1, b1, W2, b2):
        import jax, jax.numpy as jnp
        import numpy as np
        B, T, D, H, E = (16, 512, 256, 512, 8)
        Bb, Tt, Dd = x.shape
        Ee = gate_w.shape[1]
        xf = x.reshape(-1, Dd)
        N = xf.shape[0]
        logits = xf @ gate_w + gate_b
        probs = jax.nn.softmax(logits, axis=-1)
        top2_vals, top2_idx = jax.lax.top_k(probs, 2)
        cw = jnp.zeros((N, Ee), dtype=xf.dtype).at[jnp.arange(N)[:, None], top2_idx].add(top2_vals)

        def step(acc, params):
            w1, bb1, w2, bb2, we = params
            h = jax.nn.gelu(xf @ w1 + bb1, approximate=False)
            y = h @ w2 + bb2
            return (acc + we[:, None] * y, None)
        out, _ = jax.lax.scan(step, jnp.zeros_like(xf), (W1, b1, W2, b2, cw.T))
        return out.reshape(Bb, Tt, Dd)
    edge_index = jnp.stack([src, dst])
    x = x + _L0_gnn_ref(_layernorm(x, axis=-1), src, dst, edge_weight, L0_gnn_weight)
    x = x + _L0_ffn_ref(_layernorm(x, axis=-1)[None], L0_ffn_Wr, L0_ffn_br, L0_ffn_W1, L0_ffn_b1, L0_ffn_W2, L0_ffn_b2, L0_ffn_gamma, L0_ffn_beta)[0]
    x = x + _L1_gnn_ref(_layernorm(x, axis=-1), L1_gnn_W, L1_gnn_W_root, L1_gnn_bias, edge_index, edge_type_8)
    x = x + _L1_ffn_ref(_layernorm(x, axis=-1)[None], L1_ffn_gate_w, L1_ffn_gate_b, L1_ffn_W1, L1_ffn_b1, L1_ffn_W2, L1_ffn_b2)[0]
    return x

_drawn_inputs = setup_inputs


def setup_inputs(seed=0):
    import zlib

    import numpy as np

    out = dict(_drawn_inputs(seed))
    spreads = {'L0_ffn_br': (0.0, 0.1),
     'L0_ffn_b1': (0.0, 0.548),
     'L0_ffn_b2': (0.0, 0.367),
     'L0_ffn_gamma': (1.0, 0.2),
     'L0_ffn_beta': (0.0, 0.1),
     'L1_ffn_gate_b': (0.0, 0.8),
     'L1_ffn_b1': (0.0, 0.8),
     'L1_ffn_b2': (0.0, 0.8)}
    factors = {'L0_ffn_Wr': 8.0,
     'L1_gnn_bias': 8.0,
     'L1_ffn_gate_w': 6.746,
     'L1_ffn_W1': 8.0,
     'L1_ffn_W2': 8.0}
    for name, (base, spread) in spreads.items():
        noise = np.random.default_rng([zlib.crc32(name.encode()), seed]).standard_normal(out[name].shape)
        drawn = base * np.exp(spread * noise) if base else spread * noise
        out[name] = jnp.asarray(drawn.astype(out[name].dtype))
    for name, factor in factors.items():
        out[name] = (out[name] * factor).astype(out[name].dtype)
    return out
```

```python
from contextlib import ExitStack

import concourse.bass as bass
from concourse import mybir

P = 128
N = 6250
D = 256
KD = D // P
NT = 50
NP = NT * P
NB = NT // 2
TOK = 2 * P
EDGES = 200000
GE = 4 * P
NG = 392
RING = 4
R = 8
NE = 8
F = 512
KF = F // P
GW = D + R
EPS = 1e-5
PAD_NODE = N
CAPACITY = float(-(-N * 5 // (4 * NE)))

ALU = mybir.AluOpType
ACT = mybir.ActivationFunctionType
AX = mybir.AxisListType
F32 = mybir.dt.float32
BF16 = mybir.dt.bfloat16
I32 = mybir.dt.int32


def gnn_ffn_two_layers(nc, x, src, dst, typ, wgt, dst_flat, typ_flat, W_gnn0, Wr, br, W1_0, b1_0, W2_0, b2_0,
                       gamma, beta, W_rel, W_root, bias1, gate_w, gate_b, W1_1, b1_1, W2_1, b2_1, out):
    table0 = nc.dram_tensor("table0", (NP, D), F32, kind="Internal").ap()
    table1 = nc.dram_tensor("table1", (NP * R, D), F32, kind="Internal").ap()
    x2_dram = nc.dram_tensor("x2_dram", (NP, D), F32, kind="Internal").ap()
    range_dram = nc.dram_tensor("range_dram", (NG, 2), I32, kind="Internal").ap()

    def tiles_of(t):
        return t.rearrange("(t p) d -> p t d", p=P)

    ctx = ExitStack()
    with ctx:
        def sem(name):
            return ctx.enter_context(nc.semaphore(name))

        def sb(name, shape, dt=F32, scope=ctx):
            return scope.enter_context(nc.sbuf_tensor(name, shape, dt))

        wx = sb("wx", [P, 2 * NE * KD * F])
        X = wx[:, 0:NT * D].rearrange("p (t d) -> p t d", t=NT)
        spare = wx[:, NT * D:]
        typ_i = spare[:, 0:NG * 4].bitcast(I32)
        dst_i = spare[:, NG * 4:2 * NG * 4].bitcast(I32)
        Wsel1 = spare[:, 0:2 * KD * F].rearrange("p (s k f) -> p s k f", s=2, k=KD)
        W1e = wx[:, 0:NE * KD * F].rearrange("p (e k f) -> p e k f", e=NE, k=KD)
        W2e = wx[:, NE * KD * F:].rearrange("p (e k d) -> p e k d", e=NE, k=KF)
        acc = sb("acc", [P, NT, GW])
        dst_f = sb("dst_f", [P, NG * 4])
        idx1 = sb("idx1", [P, (NG + RING) * 4], I32)
        invT = sb("invT", [3 * R, NP], BF16)
        tile_range = sb("tile_range", [1, NG * 2], I32)
        ident = sb("ident", [P, P])
        identb = sb("identb", [P, P], BF16)
        iota = sb("iota", [P, P])
        iota8 = sb("iota8", [P, R])
        iota_rev = sb("iota_rev", [P, R])
        lane_i = sb("lane_i", [P, 1], I32)
        lane8_i = sb("lane8_i", [P, 1], I32)
        lane8 = sb("lane8", [P, 1])
        tile_base = sb("tile_base", [P, NT])
        ones = sb("ones", [P, P])
        minus_half = sb("minus_half", [P, NT])
        stats = sb("stats", [P, 2, 6])
        mv = sb("mv", [P, NT, 2])
        var_eps = sb("var_eps", [P, NT])
        rstd = sb("rstd", [P, NT])
        rel_node = sb("rel_node", [P, 4])
        idx_slot = sb("idx_slot", [P, RING, 4], I32)
        chosen = sb("chosen", [1, 2], I32)
        gates = sb("gates", [1, 2])
        mv2 = sb("mv2", [P, 2, 2])

        with ExitStack() as edges0:
            G0 = sb("G0", [P, RING, 4, GW], F32, edges0)
            S0 = sb("S0", [P, 3, 4, P], F32, edges0)
            src_i = sb("src_i", [P, (NG + RING) * 4], I32, edges0)
            typ_f = sb("typ_f", [P, NG * 4], F32, edges0)
            w_e = sb("w_e", [P, NG * 4], F32, edges0)
            dst_rows = sb("dst_rows", [98, 4, GE], I32, edges0)
            range_n = sb("range_n", [98, 4, 2], I32, edges0)
            range_i = sb("range_i", [98, 4, 2], I32, edges0)
        with ExitStack() as update0:
            Wg = sb("Wg", [P, KD, D], F32, update0)
            aggS = sb("aggS", [P, 2, D], F32, update0)
            aggT = sb("aggT", [P, KD, 2, P], F32, update0)
            inv = sb("inv", [P, NT, R], F32, update0)
            inv3 = sb("inv3", [P, NT, 3, R], BF16, update0)
            hsum = sb("hsum", [P, D], F32, update0)
            rm = sb("rm", [P, NT], F32, update0)
            rm_sum = sb("rm_sum", [P, 1], F32, update0)
            Wr_sb = sb("Wr_sb", [P, KD, NE], F32, update0)
            br_sb = sb("br_sb", [1, NE], F32, update0)
            mean_sb = sb("mean_sb", [P, KD], F32, update0)
            gt = sb("gt", [1, 12, NE], F32, update0)
            gc = sb("gc", [1, 12], F32, update0)
        with ExitStack() as middle:
            Wrel = sb("Wrel", [P, KD, (R + 1) * D], F32, middle)
            Wsel2 = sb("Wsel2", [P, 2, KF, D], F32, middle)
            gate_b0 = sb("gate_b0", [P, 2], F32, middle)
            b1s = sb("b1s", [P, 2, KF], F32, middle)
            b2s = sb("b2s", [1, 2, D], F32, middle)
            row = sb("row", [1, 2 + D], F32, middle)
            b2g = sb("b2g", [P, D], F32, middle)
            gam = sb("gam", [P, D], F32, middle)
            bet = sb("bet", [P, D], F32, middle)
            bias_b = sb("bias_b", [P, D], F32, middle)
            h0 = sb("h0", [P, 2, D], F32, middle)
            h0T = sb("h0T", [P, KD, TOK], F32, middle)
            hT = sb("hT", [P, 2, KF, TOK], F32, middle)
            z = sb("z", [P, 2, D], F32, middle)
            hn = sb("hn", [P, 2, D], F32, middle)
            hnT = sb("hnT", [P, KD, TOK], F32, middle)
            Y = sb("Y", [P, 4, 2 * D], F32, middle)
            ln_mv = sb("ln_mv", [P, 2, 2, 2], F32, middle)
            ln_ve = sb("ln_ve", [P, 2, 2], F32, middle)
            ln_rs = sb("ln_rs", [P, 2, 2], F32, middle)
        with ExitStack() as edges1:
            G1 = sb("G1", [P, RING, 4, D], F32, edges1)
            S1 = sb("S1", [P, 3, 4, P], F32, edges1)
            typ_rows = sb("typ_rows", [3 * R, RING, GE], I32, edges1)
            TT = sb("TT", [3 * R, 2, 4, P], BF16, edges1)
        with ExitStack() as last:
            x2in = sb("x2in", [P, 2, D], F32, last)
            q = sb("q", [P, 2, D], F32, last)
            qT = sb("qT", [P, KD, TOK], F32, last)
            qh = sb("qh", [P, 2, KF, TOK], F32, last)
            gw = sb("gw", [P, KD, NE], F32, last)
            gbb = sb("gbb", [P, NE], F32, last)
            b1e = sb("b1e", [P, NE, KF], F32, last)
            b2e = sb("b2e", [NE, D], F32, last)
            gs = sb("gs", [P, 6, NT, NE], F32, last)
            gcol = sb("gcol", [P, 2, NT], F32, last)
            cwS = sb("cwS", [P, 2, NE], F32, last)
            cwT = sb("cwT", [NE, 2, P], F32, last)
            o = sb("o", [P, 2, D], F32, last)

        bank = [ctx.enter_context(nc.psum_tensor(f"bank{i}", [P, 512], F32)) for i in range(8)]

        s = {n: sem(n) for n in (
            "consts consts2 edges_in edges_ready range_ready range_out range_in x_in table0_stats table0_rstd "
            "table0_normed table0_out "
            "update_in agg_copied aggT_ps aggT_sb agg_ps x1_done x1_stats x1_rstd inv_ready invT_ps invT_sb "
            "hsum_ready mean_ps mean_sb logit_ps soft_in soft_exp chosen_ready row_ready row_ps row_sb "
            "middle_in chosen_in chosen_scaled h0_ready h0T_ps h0T_sb f1_ps f1_sb f2_ps ln1_var ln1_rstd x2_ready "
            "x2_out ln2_var ln2_rstd hn_ready hnT_ps hnT_sb y_ps y_sb root_ps root_sb "
            "experts_in last_in x2_in x3_ready x3_var x3_rstd q_ready qT_ps qT_sb lg_ps lg_sb exp_in exp_out "
            "cw_ready q2_ready q2T_ps q2T_sb cwT_ps cwT_sb bias_ps u1_ps u1_sb u2_ps u2_sb o_ready o_out "
            "pool_passed").split()}
        y_out = [sem(f"y_out{r}") for r in range(4)]
        rows_in = [sem(f"rows_in{k}") for k in range(RING)]
        gathered = [[sem(f"gathered{layer}_{k}") for k in range(RING)] for layer in range(2)]
        seg = [{n: sem(f"{n}{layer}") for n in "idx scaled S mm added Sx mmx W Wx TT".split()} for layer in range(2)]

        def group_range(eng, g):
            lo = eng.value_load(tile_range[0:1, bass.ds(g * 2, 1)], min_val=0, max_val=NT - 1)
            hi = eng.value_load(tile_range[0:1, bass.ds(g * 2 + 1, 1)], min_val=0, max_val=NT - 1)
            return lo, hi

        def pool_gather(pool, layer):
            G, slots, table = (G0, idx_slot, table0) if layer == 0 else (G1, idx_slot, table1)
            sg = seg[layer]
            with pool.Fori(0, NG // RING) as i:
                for k in range(RING):
                    pool.wait_ge(sg["added"], i * RING + (k + 1)).then_inc(s["pool_passed"], 1)
                    pool.wait_ge(sg["idx"], i * RING + (k + 1)).then_inc(s["pool_passed"], 1)
                    for j in range(4):
                        pool.indirect_dma_start(
                            G[:, k, j, 0:D], None, table[:, :],
                            bass.IndirectOffsetOnAxis(ap=slots[:, k, j:j + 1], axis=0),
                        ).then_inc(gathered[layer][k], 16)

        def act_gather(act, layer):
            G, slots, idx = (G0, idx_slot, src_i) if layer == 0 else (G1, idx_slot, idx1)
            sg = seg[layer]
            for k in range(RING):
                nc.scalar.copy(slots[:, k, :], idx[:, 4 * k:4 * k + 4]).then_inc(sg["idx"], 1)
            with act.Fori(0, NG // RING) as i:
                for k in range(RING):
                    g = i * RING + k
                    act.wait_ge(gathered[layer][k], i * 64 + 64)
                    nc.scalar.copy(slots[:, k, :], idx[:, bass.ds((g + RING) * 4, 4)]).then_inc(sg["idx"], 1)
                    if layer == 0:
                        for j in range(4):
                            last = nc.scalar.activation(G[:, k, j, 0:D], G[:, k, j, 0:D], ACT.Copy,
                                                        scale=w_e[:, bass.ds(g * 4 + j, 1)])
                        last.then_inc(sg["scaled"], 1)

        def dve_segments(dve, layer):
            G, S = (G0, S0) if layer == 0 else (G1, S1)
            sg = seg[layer]
            dve.drain().then_inc(sg["added"], RING)
            dve.reg_mov(extra_dve, 0)

            def one_hot(g, t, slot, w_done):
                dve.drain()
                nc.vector.tensor_scalar(rel_node[:, :], dst_f[:, bass.ds(g * 4, 4)], tile_base[:, bass.ds(t, 1)],
                                        None, ALU.subtract)
                dve.drain()
                if layer == 0:
                    return nc.vector.tensor_tensor(
                        S[:, slot, :, :], iota[:, :].unsqueeze(1).to_broadcast([P, 4, P]),
                        rel_node[:, :].unsqueeze(2).to_broadcast([P, 4, P]), ALU.is_equal)
                w_done()
                for j in range(4):
                    last = nc.vector.scalar_tensor_tensor(
                        out=S[:, slot, j, :], in0=iota[:, :], scalar=rel_node[:, j:j + 1],
                        in1=bank[3][:, j * P:(j + 1) * P], op0=ALU.is_equal, op1=ALU.mult)
                return last

            def add(ps, t):
                w = GW if layer == 0 else D
                return nc.vector.tensor_tensor(acc[:, bass.ds(t, 1), 0:w].rearrange("p a d -> p (a d)"),
                                               acc[:, bass.ds(t, 1), 0:w].rearrange("p a d -> p (a d)"),
                                               ps[:, 0:w], ALU.add)

            with dve.Fori(0, NG // RING) as i:
                los = []
                for k in range(RING + 1):
                    if k < RING:
                        g = i * RING + k
                        lo, hi = group_range(dve, g)
                        los.append(lo)
                        if layer == 0:
                            nc.vector.tensor_tensor(
                                G[:, k, :, D:GW], iota8[:, :].unsqueeze(1).to_broadcast([P, 4, R]),
                                typ_f[:, bass.ds(g * 4, 4)].unsqueeze(2).to_broadcast([P, 4, R]), ALU.is_equal)
                        else:
                            dve.wait_ge(rows_in[k], i * 16 + 16)
                            nc.vector.tensor_scalar(TT[:, k % 2, :, :].rearrange("p j e -> p (j e)"),
                                                    typ_rows[:, k, :], lane8[0:3 * R, :], None,
                                                    ALU.is_equal).then_inc(sg["TT"], 1)
                        one_hot(g, lo, k % 2, lambda: dve.wait_ge(sg["W"], i * RING + (k + 1))).then_inc(sg["S"], 1)
                        with dve.If(hi > lo):
                            with dve.Fori(lo + 1, hi + 1) as t:
                                dve.reg_add(extra_dve, extra_dve, 1)
                                n = dve.snap(extra_dve, min_val=1, max_val=NG * NT)
                                one_hot(g, t, 2, lambda: dve.wait_ge(sg["Wx"], n)).then_inc(sg["Sx"], 1)
                                dve.drain()
                                dve.wait_ge(sg["mmx"], n)
                                add(bank[2], t)
                                dve.drain()
                    if k >= 1:
                        dve.drain()
                        dve.wait_ge(sg["mm"], i * RING + k)
                        add(bank[(k - 1) % 2], los[k - 1]).then_inc(sg["added"], 1)

        def pe_segments(pe, layer):
            G, S = (G0, S0) if layer == 0 else (G1, S1)
            sg = seg[layer]
            w = GW if layer == 0 else D
            pe.reg_mov(extra_pe, 0)

            def weights(t, slot):
                for j in range(4):
                    last = pe.matmul(bank[3][:, j * P:(j + 1) * P], TT[:, slot, j, :],
                                     invT[:, bass.ds(t * P, P)], start=True, stop=True)
                return last

            def product(ps, slot, k):
                for j in range(4):
                    last = pe.matmul(ps[:, 0:w], S[:, slot, j, :], G[:, k, j, 0:w], start=(j == 0), stop=(j == 3))
                return last

            with pe.Fori(0, NG // RING) as i:
                for k in range(RING):
                    g = i * RING + k
                    lo, hi = group_range(pe, g)
                    if layer == 1:
                        pe.wait_ge(sg["TT"], g + 1)
                        weights(lo, k % 2).then_inc(sg["W"], 1)
                        pe.wait_ge(gathered[1][k], i * 64 + 64)
                    else:
                        pe.wait_ge(sg["scaled"], g + 1)
                    pe.wait_ge(sg["S"], g + 1)
                    pe.wait_ge(sg["added"], g + (RING - 1))
                    product(bank[k % 2], k % 2, k).then_inc(sg["mm"], 1)
                    with pe.If(hi > lo):
                        with pe.Fori(lo + 1, hi + 1) as t:
                            pe.reg_add(extra_pe, extra_pe, 1)
                            n = pe.snap(extra_pe, min_val=1, max_val=NG * NT)
                            if layer == 1:
                                weights(t, k % 2).then_inc(sg["Wx"], 1)
                            pe.wait_ge(sg["Sx"], n)
                            product(bank[2], 2, k).then_inc(sg["mmx"], 1)

        extra_dve = nc.vector.alloc_register("extra_dve")
        extra_pe = nc.tensor.alloc_register("extra_pe")

        block = ctx.enter_context(nc.Block())

        @block.gpsimd
        def _(pool):
            g = nc.gpsimd
            g.memset(ident[:, :], 0.0).then_inc(s["consts"], 1)
            g.memset(ones[:, :], 1.0).then_inc(s["consts"], 1)
            g.memset(minus_half[:, :], -0.5).then_inc(s["consts"], 1)
            for t, step, num, base, lanes in ((iota, 1, P, 0, 0), (iota8, 1, R, 0, 0), (iota_rev, -1, R, R, 0),
                                              (tile_base, P, NT, 0, 0), (lane_i, 0, 1, 0, 1)):
                g.iota(t[:, :], pattern=[[step, num]], base=base, channel_multiplier=lanes,
                       allow_small_or_imprecise_dtypes=True).then_inc(s["consts"], 1)
            pool.wait_ge(s["consts"], 8)
            g.affine_select(out=ident[:, :], in_=ident[:, :], compare_op=ALU.not_equal, fill=1.0, base=0,
                            pattern=[[-1, P]], channel_multiplier=1).then_inc(s["consts"], 1)
            pool.wait_ge(s["table0_stats"], 1)
            g.tensor_tensor(rstd[:, :], var_eps[:, :], minus_half[:, :], ALU.pow).then_inc(s["table0_rstd"], 1)
            pool.wait_ge(s["table0_out"], 16)
            pool_gather(pool, 0)
            pool.wait_ge(s["x1_stats"], 1)
            g.tensor_tensor(rstd[:, :], var_eps[:, :], minus_half[:, :], ALU.pow).then_inc(s["x1_rstd"], 1)
            with pool.Fori(0, NB) as b:
                for n, var, out_sem in ((0, s["ln1_var"], s["ln1_rstd"]), (1, s["ln2_var"], s["ln2_rstd"])):
                    pool.wait_ge(var, b + 1)
                    g.tensor_tensor(ln_rs[:, n, :], ln_ve[:, n, :], minus_half[:, 0:2], ALU.pow).then_inc(out_sem, 1)
            for r in range(4):
                pool.wait_ge(y_out[r], 16 * (NT + 1))
            pool_gather(pool, 1)
            pool.wait_ge(s["x3_var"], 1)
            g.tensor_tensor(rstd[:, :], var_eps[:, :], minus_half[:, :], ALU.pow).then_inc(s["x3_rstd"], 1)

        @block.sync
        def _(sp):
            for r in range(4):
                sp.sem_inc(y_out[r], 16)
            sp.sem_inc(s["o_out"], 16)
            sp.dma_start(dst_rows[:, :, :], dst_flat.rearrange("(a r c) -> r a c", a=4, c=GE)).then_inc(s["range_in"], 16)
            sp.dma_start(X, tiles_of(x)).then_inc(s["x_in"], 16)
            sp.dma_start(src_i[:, :], src).then_inc(s["edges_in"], 16)
            sp.dma_start(dst_i, dst).then_inc(s["edges_in"], 16)
            sp.dma_start(typ_i, typ).then_inc(s["edges_in"], 16)
            sp.dma_start(w_e[:, :], wgt).then_inc(s["edges_in"], 16)
            sp.wait_ge(s["range_ready"], 1)
            sp.dma_start(range_dram.rearrange("(a r) c -> r a c", a=4), range_i[:, :, :]).then_inc(s["range_out"], 16)
            sp.wait_ge(s["range_out"], 16)
            sp.dma_start(tile_range[:, :], range_dram.rearrange("(a g) c -> a (g c)", a=1)).then_inc(s["range_in"], 16)
            sp.wait_ge(s["table0_normed"], 1)
            sp.dma_start(tiles_of(table0), acc[:, :, 0:D]).then_inc(s["table0_out"], 16)
            sp.wait_ge(seg[0]["added"], NG + RING)
            sp.dma_start(Wg[:, :, :], W_gnn0.rearrange("(k p) n -> p k n", p=P)).then_inc(s["update_in"], 16)
            sp.dma_start(Wr_sb[:, :, :], Wr.rearrange("(k p) n -> p k n", p=P)).then_inc(s["update_in"], 16)
            sp.dma_start(br_sb[:, :], br.rearrange("(a n) -> a n", a=1)).then_inc(s["update_in"], 16)
            sp.wait_ge(s["chosen_ready"], 1)
            for n in range(2):
                e = sp.value_load(chosen[0:1, n:n + 1], min_val=0, max_val=NE - 1)
                sp.dma_start(Wsel1[:, n, :, :], W1_0[bass.ds(e, 1), :, :].rearrange("a (k p) f -> p (a k) f", p=P)
                             ).then_inc(s["chosen_in"], 16)
                sp.dma_start(Wsel2[:, n, :, :], W2_0[bass.ds(e, 1), :, :].rearrange("a (k p) d -> p (a k) d", p=P)
                             ).then_inc(s["chosen_in"], 16)
                sp.dma_start(b1s[:, n, :], b1_0[bass.ds(e, 1), :, :].rearrange("a p k -> p (a k)")
                             ).then_inc(s["chosen_in"], 16)
                sp.dma_start(b2s[:, n, :], b2_0[bass.ds(e, 1), :]).then_inc(s["chosen_in"], 16)
            for t, v in ((gam, gamma), (bet, beta), (bias_b, bias1)):
                sp.dma_start(t[:, :], v.rearrange("(a n) -> a n", a=1).to_broadcast([P, D])).then_inc(s["middle_in"], 16)
            for r in range(R):
                sp.dma_start(Wrel[:, :, r * D:(r + 1) * D], W_rel[r].rearrange("(k p) n -> p k n", p=P)
                             ).then_inc(s["middle_in"], 16)
            sp.dma_start(Wrel[:, :, R * D:], W_root.rearrange("(k p) n -> p k n", p=P)).then_inc(s["middle_in"], 16)
            with sp.Fori(0, NB) as b:
                sp.wait_ge(s["x2_ready"], b + 1)
                sp.dma_start(tiles_of(x2_dram)[:, bass.ds(b * 2, 2), :], X[:, bass.ds(b * 2, 2), :]).then_inc(s["x2_out"], 16)
                for t in range(2):
                    for r in range(4):
                        sp.wait_ge(s["y_sb"], b * 8 + (4 * t + r + 3))
                        sp.dma_start(table1.rearrange("(t p r) d -> p t (r d)", p=P, r=R)
                                     [:, bass.ds(b * 2 + t, 1), r * 2 * D:(r + 1) * 2 * D].rearrange("p a d -> p (a d)"),
                                     Y[:, r, :]).then_inc(y_out[r], 16)
            sp.wait_ge(s["x2_out"], 16 * NB)
            sp.wait_ge(s["root_sb"], NT + 2)
            for e in range(NE):
                sp.dma_start(W1e[:, e, :, :], W1_1[e].rearrange("(k p) f -> p k f", p=P)).then_inc(s["experts_in"], 16)
                sp.dma_start(W2e[:, e, :, :], W2_1[e].rearrange("(k p) d -> p k d", p=P)).then_inc(s["experts_in"], 16)
            for r in range(4):
                sp.wait_ge(y_out[r], 16 * (NT + 1))
            with sp.Fori(0, NG // RING) as i:
                for k in range(RING):
                    sp.wait_ge(seg[1]["added"], i * RING + (k + 1))
                    sp.dma_start(typ_rows[:, k, :], typ_flat.rearrange("(a g) -> a g", a=1)
                                 [:, bass.ds(i * (RING * GE) + k * GE, GE)].to_broadcast([3 * R, GE])
                                 ).then_inc(rows_in[k], 16)
            sp.wait_ge(seg[1]["added"], NG + RING)
            sp.dma_start(gw[:, :, :], gate_w.rearrange("(k p) n -> p k n", p=P)).then_inc(s["last_in"], 16)
            sp.dma_start(gbb[:, :], gate_b.rearrange("(a n) -> a n", a=1).to_broadcast([P, NE])).then_inc(s["last_in"], 16)
            sp.dma_start(b1e[:, :, :], b1_1.rearrange("e p k -> p e k")).then_inc(s["last_in"], 16)
            sp.dma_start(b2e[:, :], b2_1).then_inc(s["last_in"], 16)
            with sp.Fori(0, NB) as b:
                sp.wait_ge(s["x3_ready"], b + 1)
                sp.dma_start(x2in[:, :, :], tiles_of(x2_dram)[:, bass.ds(b * 2, 2), :]).then_inc(s["x2_in"], 16)
            with sp.Fori(0, NB) as b:
                sp.wait_ge(s["o_ready"], b + 1)
                sp.dma_start(tiles_of(out)[:, bass.ds(b * 2, 2), :], o[:, :, :]).then_inc(s["o_out"], 16)
            sp.wait_ge(s["o_out"], 16 * (NB + 1))

        @block.scalar
        def _(act):
            act.wait_ge(s["edges_in"], 64)
            act_gather(act, 0)
            act.wait_ge(seg[0]["added"], NG + RING)
            with act.Fori(0, NB) as b:
                act.wait_ge(s["aggT_ps"], b + 1)
                nc.scalar.copy(aggS[:, :, :], acc[:, bass.ds(b * 2, 2), 0:D]).then_inc(s["agg_copied"], 1)
            for c in range(7):
                act.wait_ge(s["invT_ps"], c + 1)
                n = min(8, NT - 8 * c)
                nc.scalar.copy(invT[:, 8 * c * P:(8 * c + n) * P], bank[4 + c % 2][0:3 * R, :].bitcast(BF16)[:, 0:n * P]
                               ).then_inc(s["invT_sb"], 1)
            for n in range(3):
                act.wait_ge(s["soft_in"], n + 1)
                w = NE if n < 2 else 1
                nc.scalar.activation(gt[:, 1, 0:w], gt[:, 0, 0:w], ACT.Exp).then_inc(s["soft_exp"], 1)
            act.wait_ge(s["row_sb"], 1)
            act.wait_ge(s["chosen_in"], 16 * 8)
            for n in range(2):
                nc.scalar.activation(Wsel2[:, n, :, :], Wsel2[:, n, :, :], ACT.Copy, scale=gate_b0[:, n:n + 1]
                                     ).then_inc(s["chosen_scaled"], 1)
            with act.Fori(0, NB) as b:
                act.wait_ge(s["h0T_ps"], b + 1)
                nc.scalar.copy(h0T[:, :, :].rearrange("p k t -> p (k t)"), bank[0][:, :]).then_inc(s["h0T_sb"], 1)
                for u in range(4):
                    act.wait_ge(s["f1_ps"], b * 4 + (u + 1))
                    for v in range(2):
                        n, f = divmod(2 * u + v, KF)
                        gelu = nc.scalar.activation(hT[:, n, f, :], bank[1 + u % 2][:, v * TOK:(v + 1) * TOK],
                                                    ACT.Gelu, bias=b1s[:, n, f:f + 1])
                    gelu.then_inc(s["f1_sb"], 1)
                act.wait_ge(s["hnT_ps"], b + 1)
                nc.scalar.copy(hnT[:, :, :].rearrange("p k t -> p (k t)"), bank[0][:, :]).then_inc(s["hnT_sb"], 1)
                for t in range(2):
                    for r in range(4):
                        act.wait_ge(y_out[r], b * 32 + (16 * t + 16))
                        act.wait_ge(s["y_ps"], b * 8 + (4 * t + r + 1))
                        nc.scalar.copy(Y[:, r, :], bank[4 + r % 2][:, :]).then_inc(s["y_sb"], 1)
            act_gather(act, 1)
            with act.Fori(0, NB) as b:
                act.wait_ge(s["qT_ps"], b + 1)
                nc.scalar.copy(qT[:, :, :].rearrange("p k t -> p (k t)"), bank[0][:, :]).then_inc(s["qT_sb"], 1)
            act.wait_ge(s["exp_in"], 1)
            nc.scalar.activation(gs[:, 1, :, :], gs[:, 0, :, :], ACT.Exp).then_inc(s["exp_out"], 1)
            act.wait_ge(s["last_in"], 64)
            with act.Fori(0, NB) as b:
                act.wait_ge(s["q2T_ps"], b + 1)
                nc.scalar.copy(qT[:, :, :].rearrange("p k t -> p (k t)"), bank[0][:, :]).then_inc(s["q2T_sb"], 1)
                for e in range(NE):
                    for u in range(2):
                        act.wait_ge(s["u1_ps"], b * (2 * NE) + (2 * e + u + 1))
                        for v in range(2):
                            f = 2 * u + v
                            gelu = nc.scalar.activation(qh[:, e % 2, f, :], bank[1 + u][:, v * TOK:(v + 1) * TOK],
                                                        ACT.Gelu, bias=b1e[:, e, f:f + 1])
                        gelu.then_inc(s["u1_sb"], 1)

        @block.tensor
        def _(pe):
            pe.sem_inc(s["aggT_ps"], 1)
            pe.wait_ge(s["consts2"], 1)
            pe.wait_ge(s["range_in"], 32)
            pe_segments(pe, 0)
            pe.wait_ge(s["update_in"], 48)

            def transposes(ps, tiles, count):
                for t in range(2):
                    for k in range(KD):
                        last = pe.transpose(ps[:, (2 * k + t) * P:(2 * k + t + 1) * P], tiles[:, t, k * P:(k + 1) * P],
                                            ident[:, :])
                return last.then_inc(count, 1)

            with pe.Fori(0, NB) as b:
                pe.wait_ge(s["agg_copied"], b + 1)
                transposes(bank[0], aggS, s["aggT_ps"])
                pe.wait_ge(s["aggT_sb"], b + 1)
                for t in range(2):
                    for k in range(KD):
                        mm = pe.matmul(bank[1][:, t * D:(t + 1) * D], aggT[:, k, t, :], Wg[:, k, :],
                                       start=(k == 0), stop=(k == KD - 1))
                mm.then_inc(s["agg_ps"], 1)
            pe.wait_ge(s["inv_ready"], 1)
            for c in range(7):
                if c >= 2:
                    pe.wait_ge(s["invT_sb"], c - 1)
                for t in range(8 * c, min(8 * c + 8, NT)):
                    tr = pe.transpose(bank[4 + c % 2][0:3 * R, :].bitcast(BF16)[:, (t % 8) * P:(t % 8 + 1) * P],
                                      inv3[:, t, :, :].rearrange("p a r -> p (a r)"), identb[:, :])
                tr.then_inc(s["invT_ps"], 1)
            pe.wait_ge(s["hsum_ready"], 1)
            for k in range(KD):
                mm = pe.matmul(bank[6][:, k:k + 1], hsum[:, k * P:(k + 1) * P], ones[:, 0:1], start=True, stop=True)
            mm.then_inc(s["mean_ps"], 1)
            pe.wait_ge(s["mean_sb"], 1)
            for k in range(KD):
                mm = pe.matmul(bank[7][0:1, 0:NE], mean_sb[:, k:k + 1], Wr_sb[:, k, :], start=(k == 0), stop=(k == KD - 1))
            mm.then_inc(s["logit_ps"], 1)
            pe.wait_ge(s["row_ready"], 1)
            pe.matmul(bank[6][:, 0:2 + D], ones[0:1, :], row[0:1, :], start=True, stop=True).then_inc(s["row_ps"], 1)
            pe.wait_ge(s["chosen_in"], 16 * 8)
            pe.wait_ge(s["middle_in"], 16 * (R + 4))
            pe.wait_ge(s["chosen_scaled"], 2)
            with pe.Fori(0, NB) as b:
                pe.wait_ge(s["h0_ready"], b + 1)
                transposes(bank[0], h0, s["h0T_ps"])
                pe.wait_ge(s["h0T_sb"], b + 1)
                for u in range(4):
                    if u >= 2:
                        pe.wait_ge(s["f1_sb"], b * 4 + (u - 1))
                    for v in range(2):
                        n, f = divmod(2 * u + v, KF)
                        for k in range(KD):
                            mm = pe.matmul(bank[1 + u % 2][:, v * TOK:(v + 1) * TOK],
                                           Wsel1[:, n, k, f * P:(f + 1) * P], h0T[:, k, :],
                                           start=(k == 0), stop=(k == KD - 1))
                    mm.then_inc(s["f1_ps"], 1)
                pe.wait_ge(s["f1_sb"], b * 4 + 4)
                for t in range(2):
                    for n in range(2):
                        for f in range(KF):
                            mm = pe.matmul(bank[3][:, t * D:(t + 1) * D], hT[:, n, f, t * P:(t + 1) * P],
                                           Wsel2[:, n, f, :], start=(n == 0 and f == 0), stop=(n == 1 and f == KF - 1))
                mm.then_inc(s["f2_ps"], 1)
                pe.wait_ge(s["hn_ready"], b + 1)
                transposes(bank[0], hn, s["hnT_ps"])
                pe.wait_ge(s["hnT_sb"], b + 1)
                for t in range(2):
                    for r in range(4):
                        pe.wait_ge(s["y_sb"], b * 8 + (4 * t + r + 1))
                        for k in range(KD):
                            mm = pe.matmul(bank[4 + r % 2][:, :], hnT[:, k, t * P:(t + 1) * P],
                                           Wrel[:, k, r * 2 * D:(r + 1) * 2 * D], start=(k == 0), stop=(k == KD - 1))
                        mm.then_inc(s["y_ps"], 1)
                    pe.wait_ge(s["root_sb"], b * 2 + (t + 1))
                    for k in range(KD):
                        mm = pe.matmul(bank[6 + t][:, 0:D], hnT[:, k, t * P:(t + 1) * P], Wrel[:, k, R * D:],
                                       start=(k == 0), stop=(k == KD - 1))
                    mm.then_inc(s["root_ps"], 1)
            pe_segments(pe, 1)
            pe.wait_ge(s["last_in"], 64)
            pe.wait_ge(s["experts_in"], 16 * 2 * NE)
            with pe.Fori(0, NB) as b:
                pe.wait_ge(s["q_ready"], b + 1)
                transposes(bank[0], q, s["qT_ps"])
                pe.wait_ge(s["qT_sb"], b + 1)
                for t in range(2):
                    for k in range(KD):
                        mm = pe.matmul(bank[7][:, t * NE:(t + 1) * NE], qT[:, k, t * P:(t + 1) * P], gw[:, k, :],
                                       start=(k == 0), stop=(k == KD - 1))
                mm.then_inc(s["lg_ps"], 1)
            with pe.Fori(0, NB) as b:
                pe.wait_ge(s["q2_ready"], b + 1)
                transposes(bank[0], q, s["q2T_ps"])
                for t in range(2):
                    tr = pe.transpose(bank[7][0:NE, t * P:(t + 1) * P], cwS[:, t, :], ident[:, :])
                tr.then_inc(s["cwT_ps"], 1)
                pe.wait_ge(s["cwT_sb"], b + 1)
                for t in range(2):
                    mm = pe.matmul(bank[6][:, t * D:(t + 1) * D], cwT[:, t, :], b2e[:, :], start=True, stop=True)
                mm.then_inc(s["bias_ps"], 1)
                pe.wait_ge(s["q2T_sb"], b + 1)

                def hidden(e):
                    for u in range(2):
                        pe.wait_ge(s["u1_sb"], b * (2 * NE) + (2 * e + u + 1))
                        for v in range(2):
                            f = 2 * u + v
                            for k in range(KD):
                                mm = pe.matmul(bank[1 + u][:, v * TOK:(v + 1) * TOK], W1e[:, e, k, f * P:(f + 1) * P],
                                               qT[:, k, :], start=(k == 0), stop=(k == KD - 1))
                        mm.then_inc(s["u1_ps"], 1)

                def output(e):
                    pe.wait_ge(s["u1_sb"], b * (2 * NE) + (2 * e + 4))
                    pe.wait_ge(s["u2_sb"], b * NE + (e + 1))
                    for t in range(2):
                        for f in range(KF):
                            mm = pe.matmul(bank[3 + e % 2][:, t * D:(t + 1) * D], qh[:, e % 2, f, t * P:(t + 1) * P],
                                           W2e[:, e, f, :], start=(f == 0), stop=(f == KF - 1))
                    mm.then_inc(s["u2_ps"], 1)

                for e in range(NE + 1):
                    if e < NE:
                        hidden(e)
                    if e >= 1:
                        output(e - 1)

        @block.vector
        def _(dve):
            v = nc.vector
            dve.drain().then_inc(s["y_sb"], 2)
            dve.drain().then_inc(s["root_sb"], 2)
            dve.drain().then_inc(s["u1_sb"], 2)
            dve.drain().then_inc(s["u2_sb"], 2)

            def row_stats(rows, b):
                for t in range(2):
                    v.bn_stats(stats[:, t, :], rows[:, bass.ds(b * 2 + t, 1), 0:D].rearrange("p a d -> p (a d)"))
                dve.drain()
                for t in range(2):
                    v.bn_aggr(mv2[:, t, :], stats[:, t, :])
                dve.drain()
                v.tensor_copy(mv[:, bass.ds(b * 2, 2), :], mv2[:, :, :])

            dve.wait_ge(s["consts"], 9)
            v.tensor_copy(identb[:, :], ident[:, :])
            v.tensor_scalar(lane8_i[:, :], lane_i[:, :], R - 1, None, ALU.bitwise_and)
            dve.drain()
            v.tensor_copy(lane8[:, :], lane8_i[:, :]).then_inc(s["consts2"], 1)
            dve.wait_ge(s["range_in"], 16)
            v.tensor_reduce(range_n[:, :, 0:1], dst_rows[:, :, :], AX.X, ALU.min)
            v.tensor_reduce(range_n[:, :, 1:2], dst_rows[:, :, :], AX.X, ALU.max)
            dve.drain()
            v.tensor_scalar(range_i[:, :, :], range_n[:, :, :], 7, None, ALU.arith_shift_right).then_inc(s["range_ready"], 1)
            dve.wait_ge(s["x_in"], 16)
            with dve.Fori(0, NB) as b:
                row_stats(X, b)
            dve.drain()
            v.tensor_scalar(var_eps[:, :], mv[:, :, 1], EPS, None, ALU.add).then_inc(s["table0_stats"], 1)
            dve.wait_ge(s["table0_rstd"], 1)
            with dve.Fori(0, NT) as t:
                v.tensor_scalar(acc[:, bass.ds(t, 1), 0:D].rearrange("p a d -> p (a d)"),
                                X[:, bass.ds(t, 1), :].rearrange("p a d -> p (a d)"),
                                mv[:, bass.ds(t, 1), 0:1].rearrange("p a d -> p (a d)"), rstd[:, bass.ds(t, 1)],
                                ALU.subtract, ALU.mult)
            dve.drain().then_inc(s["table0_normed"], 1)
            dve.wait_ge(s["edges_in"], 64)
            v.tensor_copy(dst_f[:, :], dst_i)
            v.tensor_copy(typ_f[:, :], typ_i)
            v.memset(idx1[:, NG * 4:], 0)
            v.scalar_tensor_tensor(out=idx1[:, 0:NG * 4], in0=src_i[:, 0:NG * 4], scalar=float(R), in1=typ_i,
                                   op0=ALU.mult, op1=ALU.add)
            dve.wait_ge(s["table0_out"], 16)
            v.memset(acc[:, :, :], 0.0)
            dve.wait_ge(s["range_in"], 32)
            dve.drain()
            dve_segments(dve, 0)

            with dve.Fori(0, NB) as b:
                dve.wait_ge(s["aggT_ps"], b + 2)
                v.tensor_copy(aggT[:, :, :, :].rearrange("p k t c -> p (k t c)"), bank[0][:, :]).then_inc(s["aggT_sb"], 1)
                dve.wait_ge(s["agg_ps"], b + 1)
                v.tensor_tensor(X[:, bass.ds(b * 2, 2), :], X[:, bass.ds(b * 2, 2), :],
                                bank[1][:, :].rearrange("p (t d) -> p t d", t=2), ALU.add)
                dve.drain()
                row_stats(X, b)
            dve.drain()
            v.tensor_scalar(var_eps[:, :], mv[:, :, 1], EPS, None, ALU.add).then_inc(s["x1_stats"], 1)
            v.tensor_scalar(inv[:, :, :], acc[:, :, D:GW], 1.0, None, ALU.max)
            dve.drain()
            v.reciprocal(inv[:, :, :], inv[:, :, :])
            for part in range(3):
                dve.drain()
                v.tensor_copy(inv3[:, :, part, :], inv[:, :, :])
                if part < 2:
                    dve.drain()
                    v.tensor_tensor(inv[:, :, :], inv[:, :, :], inv3[:, :, part, :], ALU.subtract)
            dve.drain().then_inc(s["inv_ready"], 1)
            dve.wait_ge(s["x1_rstd"], 1)
            v.tensor_tensor(rm[:, :], rstd[:, :], mv[:, :, 0], ALU.mult)
            v.memset(hsum[:, :], 0.0)
            dve.drain()
            v.tensor_reduce(rm_sum[:, :], rm[:, :], AX.X, ALU.add)
            with dve.Fori(0, NT) as t:
                dve.drain()
                v.scalar_tensor_tensor(out=hsum[:, :], in0=X[:, bass.ds(t, 1), :].rearrange("p a d -> p (a d)"),
                                       scalar=rstd[:, bass.ds(t, 1)], in1=hsum[:, :], op0=ALU.mult, op1=ALU.add)
            dve.drain()
            v.tensor_scalar(hsum[:, :], hsum[:, :], rm_sum[:, :], None, ALU.subtract).then_inc(s["hsum_ready"], 1)
            dve.wait_ge(s["mean_ps"], 1)
            v.tensor_scalar(mean_sb[:, :], bank[6][:, 0:KD], 1.0 / N, None, ALU.mult).then_inc(s["mean_sb"], 1)

            def softmax(src_row, n):
                v.tensor_reduce(gc[:, 0:1], src_row, AX.X, ALU.max)
                dve.drain()
                v.tensor_scalar(gt[:, 0, :], src_row, gc[:, 0:1], None, ALU.subtract).then_inc(s["soft_in"], 1)
                dve.wait_ge(s["soft_exp"], n)
                v.tensor_reduce(gc[:, 1:2], gt[:, 1, :], AX.X, ALU.add)
                dve.drain()
                v.reciprocal(gc[:, 2:3], gc[:, 1:2])
                dve.drain()
                v.tensor_scalar(gt[:, 3, :], gt[:, 1, :], gc[:, 2:3], None, ALU.mult)
                dve.drain()

            dve.wait_ge(s["logit_ps"], 1)
            v.tensor_tensor(gt[:, 2, :], bank[7][0:1, 0:NE], br_sb[:, :], ALU.add)
            dve.drain()
            softmax(gt[:, 2, :], 1)
            v.tensor_scalar(gt[:, 4, :], gt[:, 3, :], float(N), CAPACITY, ALU.mult, ALU.max)
            dve.drain()
            v.reciprocal(gt[:, 5, :], gt[:, 4, :])
            dve.drain()
            v.scalar_tensor_tensor(out=gt[:, 6, :], in0=gt[:, 5, :], scalar=CAPACITY, in1=gt[:, 3, :],
                                   op0=ALU.mult, op1=ALU.mult)
            dve.drain()
            softmax(gt[:, 6, :], 2)
            v.tensor_copy(gt[:, 4, :], gt[:, 3, :])
            dve.drain()
            for n in range(2):
                v.tensor_reduce(gc[:, 4 + n:5 + n], gt[:, 4, :], AX.X, ALU.max)
                dve.drain()
                v.scalar_tensor_tensor(out=gt[:, 7, :], in0=gt[:, 4, :], scalar=gc[:, 4 + n:5 + n],
                                       in1=iota_rev[0:1, :], op0=ALU.is_equal, op1=ALU.mult)
                dve.drain()
                v.tensor_reduce(gc[:, 6 + n:7 + n], gt[:, 7, :], AX.X, ALU.max)
                dve.drain()
                v.tensor_scalar(gt[:, 8, :], gt[:, 7, :], gc[:, 6 + n:7 + n], None, ALU.is_equal)
                dve.drain()
                v.scalar_tensor_tensor(out=gt[:, 4, :], in0=gt[:, 8, :], scalar=-4.0, in1=gt[:, 4, :],
                                       op0=ALU.mult, op1=ALU.add)
                dve.drain()
            v.tensor_tensor(gt[:, 0, 0:1], gc[:, 5:6], gc[:, 4:5], ALU.subtract).then_inc(s["soft_in"], 1)
            dve.wait_ge(s["soft_exp"], 3)
            v.tensor_scalar(gc[:, 8:9], gt[:, 1, 0:1], 1.0, None, ALU.add)
            dve.drain()
            v.reciprocal(gc[:, 9:10], gc[:, 8:9])
            dve.drain()
            v.tensor_tensor(gc[:, 10:11], gc[:, 9:10], gt[:, 1, 0:1], ALU.mult)
            dve.wait_ge(s["invT_sb"], 7)
            dve.drain()
            v.tensor_copy(gates[:, :], gc[:, 9:11])
            v.tensor_scalar(chosen[:, :], gc[:, 6:8], -1.0, float(NE), ALU.mult, ALU.add).then_inc(s["chosen_ready"], 1)
            dve.wait_ge(s["chosen_in"], 16 * 8)
            dve.drain()
            v.tensor_copy(row[:, 0:2], gates[:, :])
            v.tensor_scalar(row[:, 2:], b2s[:, 0, :], gates[:, 0:1], None, ALU.mult)
            dve.drain()
            v.scalar_tensor_tensor(out=row[:, 2:], in0=b2s[:, 1, :], scalar=gates[:, 1:2], in1=row[:, 2:],
                                   op0=ALU.mult, op1=ALU.add)
            dve.drain().then_inc(s["row_ready"], 1)
            dve.wait_ge(s["row_ps"], 1)
            v.tensor_copy(gate_b0[:, :], bank[6][:, 0:2])
            v.tensor_copy(b2g[:, :], bank[6][:, 2:2 + D])
            dve.drain().then_inc(s["row_sb"], 1)
            dve.wait_ge(s["middle_in"], 16 * (R + 4))

            def per_tile(t):
                return t[:, :].unsqueeze(1).to_broadcast([P, 2, D])

            with dve.Fori(0, NB) as b:
                batch = bass.ds(b * 2, 2)
                for t in range(2):
                    v.tensor_scalar(h0[:, t, :], X[:, bass.ds(b * 2 + t, 1), :].rearrange("p a d -> p (a d)"),
                                    mv[:, bass.ds(b * 2 + t, 1), 0:1].rearrange("p a d -> p (a d)"),
                                    rstd[:, bass.ds(b * 2 + t, 1)], ALU.subtract, ALU.mult)
                dve.drain().then_inc(s["h0_ready"], 1)
                dve.wait_ge(s["f2_ps"], b + 1)
                v.tensor_tensor(z[:, :, :], bank[3][:, :].rearrange("p (t d) -> p t d", t=2), h0[:, :, :], ALU.add)
                dve.drain()
                v.tensor_tensor(z[:, :, :], z[:, :, :], per_tile(b2g), ALU.add)
                dve.drain()
                for n, tile, var, rs in ((0, z, s["ln1_var"], s["ln1_rstd"]), (1, None, s["ln2_var"], s["ln2_rstd"])):
                    for t in range(2):
                        a = z[:, t, :] if n == 0 else X[:, bass.ds(b * 2 + t, 1), :].rearrange("p a d -> p (a d)")
                        v.bn_stats(stats[:, t, :], a)
                    dve.drain()
                    for t in range(2):
                        v.bn_aggr(ln_mv[:, n, t, :], stats[:, t, :])
                    dve.drain()
                    v.tensor_scalar(ln_ve[:, n, :], ln_mv[:, n, :, 1], EPS, None, ALU.add).then_inc(var, 1)
                    dve.wait_ge(rs, b + 1)
                    for t in range(2):
                        a = z[:, t, :] if n == 0 else X[:, bass.ds(b * 2 + t, 1), :].rearrange("p a d -> p (a d)")
                        v.tensor_scalar((z if n == 0 else hn)[:, t, :], a, ln_mv[:, n, t, 0:1], ln_rs[:, n, t:t + 1],
                                        ALU.subtract, ALU.mult)
                    dve.drain()
                    if n == 0:
                        v.tensor_tensor(z[:, :, :], z[:, :, :], per_tile(gam), ALU.mult)
                        dve.drain()
                        v.tensor_tensor(z[:, :, :], z[:, :, :], per_tile(bet), ALU.add)
                        dve.drain()
                        v.tensor_tensor(X[:, batch, :], X[:, batch, :], z[:, :, :], ALU.add)
                        dve.drain().then_inc(s["x2_ready"], 1)
                dve.drain().then_inc(s["hn_ready"], 1)
                for t in range(2):
                    dve.wait_ge(s["root_ps"], b * 2 + (t + 1))
                    v.tensor_tensor(acc[:, bass.ds(b * 2 + t, 1), 0:D].rearrange("p a d -> p (a d)"), bank[6 + t][:, 0:D],
                                    bias_b[:, :], ALU.add).then_inc(s["root_sb"], 1)
            for r in range(4):
                dve.wait_ge(y_out[r], 16 * (NT + 1))
            dve_segments(dve, 1)

            dve.drain().then_inc(s["x3_ready"], 1)
            with dve.Fori(0, NB) as b:
                batch = bass.ds(b * 2, 2)
                dve.wait_ge(s["x2_in"], b * 16 + 16)
                v.scalar_tensor_tensor(out=acc[:, batch, 0:D], in0=acc[:, batch, 0:D], scalar=0.0, in1=x2in[:, :, :],
                                       op0=ALU.max, op1=ALU.add).then_inc(s["x3_ready"], 1)
                dve.drain()
                row_stats(acc, b)
            dve.drain()
            v.tensor_scalar(var_eps[:, :], mv[:, :, 1], EPS, None, ALU.add).then_inc(s["x3_var"], 1)
            dve.wait_ge(s["x3_rstd"], 1)

            def normed(b):
                for t in range(2):
                    v.tensor_scalar(q[:, t, :], acc[:, bass.ds(b * 2 + t, 1), 0:D].rearrange("p a d -> p (a d)"),
                                    mv[:, bass.ds(b * 2 + t, 1), 0:1].rearrange("p a d -> p (a d)"),
                                    rstd[:, bass.ds(b * 2 + t, 1)], ALU.subtract, ALU.mult)

            dve.wait_ge(s["last_in"], 64)
            with dve.Fori(0, NB) as b:
                normed(b)
                dve.drain().then_inc(s["q_ready"], 1)
                dve.wait_ge(s["lg_ps"], b + 1)
                v.tensor_tensor(gs[:, 2, bass.ds(b * 2, 2), :], bank[7][:, 0:2 * NE].rearrange("p (t e) -> p t e", t=2),
                                gbb[:, :].unsqueeze(1).to_broadcast([P, 2, NE]), ALU.add)
            dve.drain()

            def over_experts(col):
                return col.unsqueeze(2).to_broadcast([P, NT, NE])

            rev = iota_rev[:, :].unsqueeze(1).to_broadcast([P, NT, NE])
            v.tensor_reduce(gcol[:, 0, :], gs[:, 2, :, :], AX.X, ALU.max)
            dve.drain()
            v.tensor_tensor(gs[:, 0, :, :], gs[:, 2, :, :], over_experts(gcol[:, 0, :]), ALU.subtract).then_inc(s["exp_in"], 1)
            dve.wait_ge(s["exp_out"], 1)
            v.tensor_reduce(gcol[:, 0, :], gs[:, 1, :, :], AX.X, ALU.add)
            dve.drain()
            v.reciprocal(gcol[:, 1, :], gcol[:, 0, :])
            dve.drain()
            v.tensor_tensor(gs[:, 0, :, :], gs[:, 1, :, :], over_experts(gcol[:, 1, :]), ALU.mult)
            dve.drain()
            v.tensor_copy(gs[:, 1, :, :], gs[:, 0, :, :])
            for n in range(2):
                dve.drain()
                v.tensor_reduce(gcol[:, 0, :], gs[:, 1, :, :], AX.X, ALU.max)
                dve.drain()
                v.tensor_tensor(gs[:, 2, :, :], gs[:, 1, :, :], over_experts(gcol[:, 0, :]), ALU.is_equal)
                dve.drain()
                v.tensor_tensor(gs[:, 2, :, :], gs[:, 2, :, :], rev, ALU.mult)
                dve.drain()
                v.tensor_reduce(gcol[:, 1, :], gs[:, 2, :, :], AX.X, ALU.max)
                dve.drain()
                v.tensor_tensor(gs[:, 3 + n, :, :], gs[:, 2, :, :], over_experts(gcol[:, 1, :]), ALU.is_equal)
                dve.drain()
                v.scalar_tensor_tensor(out=gs[:, 1, :, :], in0=gs[:, 3 + n, :, :], scalar=-4.0, in1=gs[:, 1, :, :],
                                       op0=ALU.mult, op1=ALU.add)
            v.tensor_tensor(gs[:, 3, :, :], gs[:, 3, :, :], gs[:, 4, :, :], ALU.add)
            dve.drain()
            v.tensor_tensor(gs[:, 5, :, :], gs[:, 3, :, :], gs[:, 0, :, :], ALU.mult)
            dve.drain()
            with dve.Fori(0, NB) as b:
                batch = bass.ds(b * 2, 2)
                normed(b)
                v.tensor_copy(cwS[:, :, :], gs[:, 5, batch, :])
                dve.drain().then_inc(s["q2_ready"], 1)
                dve.wait_ge(s["cwT_ps"], b + 1)
                v.tensor_copy(cwT[:, :, :], bank[7][0:NE, 0:2 * P].rearrange("p (t c) -> p t c", t=2)).then_inc(s["cwT_sb"], 1)
                dve.drain()
                dve.wait_ge(s["bias_ps"], b + 1)
                dve.wait_ge(s["o_out"], b * 16 + 16)
                v.tensor_tensor(o[:, :, :], acc[:, batch, 0:D], bank[6][:, :].rearrange("p (t d) -> p t d", t=2), ALU.add)
                for e in range(NE):
                    dve.drain()
                    dve.wait_ge(s["u2_ps"], b * NE + (e + 1))
                    for t in range(2):
                        fma = v.scalar_tensor_tensor(out=o[:, t, :], in0=bank[3 + e % 2][:, t * D:(t + 1) * D],
                                                     scalar=cwS[:, t, e:e + 1], in1=o[:, t, :],
                                                     op0=ALU.mult, op1=ALU.add)
                    fma.then_inc(s["u2_sb"], 1)
                dve.drain().then_inc(s["o_ready"], 1)


_OUT_ROWS = (N, D)


def kernel(**inputs):
    import numpy as _np
    import concourse.bacc as _bacc
    from concourse import mybir as _mybir
    from concourse.bass_utils import run_bass_kernel_spmd as _run

    a = {k: _np.ascontiguousarray(v) for k, v in inputs.items()}
    pad = NG * GE - EDGES

    def padded(v, value, more=0):
        return _np.concatenate([v, _np.full(pad + more, value, v.dtype)])

    def by_partition(v):
        return _np.ascontiguousarray(v.reshape(-1, P).T)

    def hidden_bias(v):
        return _np.ascontiguousarray(v.reshape(NE, KF, P).transpose(0, 2, 1))

    dst_flat = padded(a["dst"], PAD_NODE)
    typ_flat = padded(a["edge_type_8"], 0)
    ins = {
        "x": _np.concatenate([a["x"], _np.zeros((NP - N, D), a["x"].dtype)]),
        "src": by_partition(padded(a["src"], 0, RING * GE)),
        "dst": by_partition(dst_flat),
        "typ": by_partition(typ_flat),
        "wgt": by_partition(padded(a["edge_weight"], 0)),
        "dst_flat": dst_flat,
        "typ_flat": typ_flat,
        "W_gnn0": a["L0_gnn_weight"],
        "Wr": a["L0_ffn_Wr"],
        "br": a["L0_ffn_br"],
        "W1_0": a["L0_ffn_W1"],
        "b1_0": hidden_bias(a["L0_ffn_b1"]),
        "W2_0": a["L0_ffn_W2"],
        "b2_0": a["L0_ffn_b2"],
        "gamma": a["L0_ffn_gamma"],
        "beta": a["L0_ffn_beta"],
        "W_rel": a["L1_gnn_W"],
        "W_root": a["L1_gnn_W_root"],
        "bias1": a["L1_gnn_bias"],
        "gate_w": a["L1_ffn_gate_w"],
        "gate_b": a["L1_ffn_gate_b"],
        "W1_1": a["L1_ffn_W1"],
        "b1_1": hidden_bias(a["L1_ffn_b1"]),
        "W2_1": a["L1_ffn_W2"],
        "b2_1": a["L1_ffn_b2"],
    }
    nc = _bacc.Bacc("TRN2", target_bir_lowering=False, num_devices=1)
    arrays, args = {}, []
    for name, v in ins.items():
        arrays[f"in_{name}"] = v
        args.append(nc.dram_tensor(f"in_{name}", v.shape, _mybir.dt.from_np(v.dtype), kind="ExternalInput").ap())
    out = nc.dram_tensor("out_0_dram", (NP, D), _mybir.dt.float32, kind="ExternalOutput").ap()
    gnn_ffn_two_layers(nc, *args, out)
    r = _run(nc, [arrays], core_ids=[0])
    return r.results[0]["out_0_dram"][:N]
```

```python
from contextlib import ExitStack

import concourse.bass as bass
from concourse import mybir

P = 128
N = 6250
D = 256
KD = D // P
NT = 50
NP = NT * P
NB = NT // 2
TOK = 2 * P
EDGES = 200000
GE = 4 * P
NG = 392
RINGS = (4, 8)
TURNS = NG // RINGS[1]
TYPE_RING = 2
R = 8
NE = 8
F = 512
KF = F // P
GW = D + R
EPS = 1e-5
PAD_NODE = N
CAPACITY = float(-(-N * 5 // (4 * NE)))

ALU = mybir.AluOpType
ACT = mybir.ActivationFunctionType
AX = mybir.AxisListType
F32 = mybir.dt.float32
BF16 = mybir.dt.bfloat16
I32 = mybir.dt.int32


def gnn_ffn_two_layers(nc, x, src, dst, typ, wgt, dst_flat, typ_flat, W_gnn0, Wr, br, W1_0, b1_0, W2_0, b2_0,
                       gamma, beta, W_rel, W_root, bias1, gate_w, gate_b, W1_1, b1_1, W2_1, b2_1, out):
    table0 = nc.dram_tensor("table0", (NP, D), F32, kind="Internal").ap()
    table1 = nc.dram_tensor("table1", (NP * R, D), F32, kind="Internal").ap()
    x2_dram = nc.dram_tensor("x2_dram", (NP, D), F32, kind="Internal").ap()
    range_dram = nc.dram_tensor("range_dram", (NG, 2), I32, kind="Internal").ap()

    def tiles_of(t):
        return t.rearrange("(t p) d -> p t d", p=P)

    ctx = ExitStack()
    with ctx:
        def sem(name):
            return ctx.enter_context(nc.semaphore(name))

        def sb(name, shape, dt=F32, scope=ctx):
            return scope.enter_context(nc.sbuf_tensor(name, shape, dt))

        wx = sb("wx", [P, 2 * NE * KD * F])
        X = wx[:, 0:NT * D].rearrange("p (t d) -> p t d", t=NT)
        spare = wx[:, NT * D:]
        typ_i = spare[:, 0:NG * 4].bitcast(I32)
        dst_i = spare[:, NG * 4:2 * NG * 4].bitcast(I32)
        Wsel1 = spare[:, 0:2 * KD * F].rearrange("p (s k f) -> p s k f", s=2, k=KD)
        W1e = wx[:, 0:NE * KD * F].rearrange("p (e k f) -> p e k f", e=NE, k=KD)
        W2e = wx[:, NE * KD * F:].rearrange("p (e k d) -> p e k d", e=NE, k=KF)
        acc = sb("acc", [P, NT, GW])
        dst_f = sb("dst_f", [P, NG * 4])
        idx1 = sb("idx1", [P, (NG + RINGS[1]) * 4], I32)
        invT = sb("invT", [3 * R, NP], BF16)
        tile_range = sb("tile_range", [1, NG * 2], I32)
        ident = sb("ident", [P, P])
        identb = sb("identb", [P, P], BF16)
        iota = sb("iota", [P, P])
        iota8 = sb("iota8", [P, R])
        iota_rev = sb("iota_rev", [P, R])
        lane_i = sb("lane_i", [P, 1], I32)
        lane8_i = sb("lane8_i", [P, 1], I32)
        lane8 = sb("lane8", [P, 1])
        tile_base = sb("tile_base", [P, NT])
        ones = sb("ones", [P, P])
        minus_half = sb("minus_half", [P, NT])
        stats = sb("stats", [P, 2, 6])
        mv = sb("mv", [P, NT, 2])
        var_eps = sb("var_eps", [P, NT])
        rstd = sb("rstd", [P, NT])
        rel_node = sb("rel_node", [P, 4])
        idx_slot = sb("idx_slot", [P, RINGS[1], 4], I32)
        turn1 = sb("turn1", [1, TURNS])
        bound = sb("bound", [1, NB])
        turn_lo = sb("turn_lo", [1, TURNS])
        turns_f = sb("turns_f", [1, NB])
        turns = sb("turns", [1, NB + 1], I32)
        chosen = sb("chosen", [1, 2], I32)
        gates = sb("gates", [1, 2])
        mv2 = sb("mv2", [P, 2, 2])

        with ExitStack() as edges0:
            G0 = sb("G0", [P, RINGS[0], 4, GW], F32, edges0)
            S0 = sb("S0", [P, 2, 4, P], F32, edges0)
            src_i = sb("src_i", [P, (NG + RINGS[0]) * 4], I32, edges0)
            typ_f = sb("typ_f", [P, NG * 4], F32, edges0)
            w_e = sb("w_e", [P, NG * 4], F32, edges0)
            dst_rows = sb("dst_rows", [98, 4, GE], I32, edges0)
            range_n = sb("range_n", [98, 4, 2], I32, edges0)
            range_i = sb("range_i", [98, 4, 2], I32, edges0)
            turn_of = sb("turn_of", [1, NB, TURNS], F32, edges0)
        with ExitStack() as update0:
            Wg = sb("Wg", [P, KD, D], F32, update0)
            aggS = sb("aggS", [P, 2, D], F32, update0)
            aggT = sb("aggT", [P, KD, 2, P], F32, update0)
            inv = sb("inv", [P, NT, R], F32, update0)
            inv3 = sb("inv3", [P, NT, 3, R], BF16, update0)
            hsum = sb("hsum", [P, D], F32, update0)
            rm = sb("rm", [P, NT], F32, update0)
            rm_sum = sb("rm_sum", [P, 1], F32, update0)
            Wr_sb = sb("Wr_sb", [P, KD, NE], F32, update0)
            br_sb = sb("br_sb", [1, NE], F32, update0)
            mean_sb = sb("mean_sb", [P, KD], F32, update0)
            gt = sb("gt", [1, 12, NE], F32, update0)
            gc = sb("gc", [1, 12], F32, update0)
        with ExitStack() as middle:
            Wrel = sb("Wrel", [P, KD, (R + 1) * D], F32, middle)
            Wsel2 = sb("Wsel2", [P, 2, KF, D], F32, middle)
            gate_b0 = sb("gate_b0", [P, 2], F32, middle)
            b1s = sb("b1s", [P, 2, KF], F32, middle)
            b2s = sb("b2s", [1, 2, D], F32, middle)
            row = sb("row", [1, 2 + D], F32, middle)
            b2g = sb("b2g", [P, D], F32, middle)
            gam = sb("gam", [P, D], F32, middle)
            bet = sb("bet", [P, D], F32, middle)
            bias_b = sb("bias_b", [P, D], F32, middle)
            h0 = sb("h0", [P, 2, D], F32, middle)
            h0T = sb("h0T", [P, KD, TOK], F32, middle)
            hT = sb("hT", [P, 2, KF, TOK], F32, middle)
            z = sb("z", [P, 2, D], F32, middle)
            hn = sb("hn", [P, 2, D], F32, middle)
            hnT = sb("hnT", [P, KD, TOK], F32, middle)
            Y = sb("Y", [P, 4, 2 * D], F32, middle)
            ln_mv = sb("ln_mv", [P, 2, 2, 2], F32, middle)
            ln_ve = sb("ln_ve", [P, 2, 2], F32, middle)
            ln_rs = sb("ln_rs", [P, 2, 2], F32, middle)
        with ExitStack() as last:
            G1 = sb("G1", [P, RINGS[1], 4, D], F32, last)
            S1 = sb("S1", [P, 2, 4, P], F32, last)
            typ_rows = sb("typ_rows", [3 * R, TYPE_RING, GE], I32, last)
            TT = sb("TT", [3 * R, 2, 4, P], BF16, last)
            q = sb("q", [P, 2, D], F32, last)
            x2in = q
            qT = sb("qT", [P, KD, TOK], F32, last)
            qh = sb("qh", [P, 2, KF, TOK], F32, last)
            gw = sb("gw", [P, KD, NE], F32, last)
            gbb = sb("gbb", [P, NE], F32, last)
            b1e = sb("b1e", [P, NE, KF], F32, last)
            b2e = sb("b2e", [NE, D], F32, last)
            logits = sb("logits", [P, 2, NE], F32, last)
            gs = sb("gs", [P, 6, 2, NE], F32, last)
            gcol = sb("gcol", [P, 2, 2], F32, last)
            cwS = sb("cwS", [P, 2, NE], F32, last)
            cwT = sb("cwT", [NE, 2, P], F32, last)
            sd = sb("sd", [P, 2], F32, last)
            rs3 = sb("rs3", [P, 2], F32, last)
            mv3 = sb("mv3", [P, 2, 2], F32, last)
            o = sb("o", [P, 2, D], F32, last)

        bank = [ctx.enter_context(nc.psum_tensor(f"bank{i}", [P, 512], F32)) for i in range(8)]

        s = {n: sem(n) for n in (
            "consts consts2 edges_in edges_ready range_ready range_out range_in x_in table0_stats table0_rstd "
            "table0_normed table0_out "
            "update_in agg_copied aggT_ps aggT_sb agg_ps x1_done x1_stats x1_rstd inv_ready invT_ps invT_sb "
            "hsum_ready mean_ps mean_sb logit_ps soft_in soft_exp chosen_ready row_ready row_ps row_sb "
            "middle_in chosen_in chosen_scaled h0_ready h0T_ps h0T_sb f1_ps f1_sb f2_ps ln1_var ln1_rstd x2_ready "
            "x2_out ln2_var ln2_rstd hn_ready hnT_ps hnT_sb y_ps y_sb root_ps root_sb "
            "experts_in last_in x2_in x3_var x3_sd q_ready qT_ps qT_sb lg_ps exp_in exp_out "
            "cw_ready cwT_ps cwT_sb bias_ps u1_ps u1_sb u2_ps u2_sb o_ready o_out "
            "pool_passed dve_passed").split()}
        y_out = [sem(f"y_out{r}") for r in range(4)]
        rows_in = [sem(f"rows_in{k}") for k in range(TYPE_RING)]
        gathered = [[sem(f"gathered{layer}_{k}") for k in range(RINGS[layer])] for layer in range(2)]
        seg = [{n: sem(f"{n}{layer}") for n in "idx scaled S mm added Sx mmx W Wx TT".split()} for layer in range(2)]

        def group_range(eng, g):
            lo = eng.value_load(tile_range[0:1, bass.ds(g * 2, 1)], min_val=0, max_val=NT - 1)
            hi = eng.value_load(tile_range[0:1, bass.ds(g * 2 + 1, 1)], min_val=0, max_val=NT - 1)
            return lo, hi

        def pool_gather(pool, layer):
            G, table, ring, sg = (G0, G1)[layer], (table0, table1)[layer], RINGS[layer], seg[layer]
            with pool.Fori(0, NG // ring) as i:
                for k in range(ring):
                    pool.wait_ge(sg["added"], i * ring + (k + 1)).then_inc(s["pool_passed"], 1)
                    pool.wait_ge(sg["idx"], i * ring + (k + 1)).then_inc(s["pool_passed"], 1)
                    for j in range(4):
                        pool.indirect_dma_start(
                            G[:, k, j, 0:D], None, table[:, :],
                            bass.IndirectOffsetOnAxis(ap=idx_slot[:, k, j:j + 1], axis=0),
                        ).then_inc(gathered[layer][k], 16)

        def act_first_rows(layer):
            for k in range(RINGS[layer]):
                nc.scalar.copy(idx_slot[:, k, :], (src_i, idx1)[layer][:, 4 * k:4 * k + 4]).then_inc(seg[layer]["idx"], 1)

        def act_turn(act, layer, i):
            idx, ring, sg = (src_i, idx1)[layer], RINGS[layer], seg[layer]
            for k in range(ring):
                g = i * ring + k
                act.wait_ge(gathered[layer][k], i * 64 + 64)
                nc.scalar.copy(idx_slot[:, k, :], idx[:, bass.ds((g + ring) * 4, 4)]).then_inc(sg["idx"], 1)
                if layer == 0:
                    for j in range(4):
                        last = nc.scalar.activation(G0[:, k, j, 0:D], G0[:, k, j, 0:D], ACT.Copy,
                                                    scale=w_e[:, bass.ds(g * 4 + j, 1)])
                    last.then_inc(sg["scaled"], 1)

        def dve_turn(dve, layer, i):
            S, ring, sg = (S0, S1)[layer], RINGS[layer], seg[layer]
            width = (GW, D)[layer]

            def one_hot(g, t, slot, inverse_counts, ps):
                dve.drain()
                nc.vector.tensor_scalar(rel_node[:, :], dst_f[:, bass.ds(g * 4, 4)], tile_base[:, bass.ds(t, 1)],
                                        None, ALU.subtract)
                dve.drain()
                if layer == 0:
                    return nc.vector.tensor_tensor(
                        S[:, slot, :, :], iota[:, :].unsqueeze(1).to_broadcast([P, 4, P]),
                        rel_node[:, :].unsqueeze(2).to_broadcast([P, 4, P]), ALU.is_equal)
                inverse_counts()
                for j in range(4):
                    last = nc.vector.scalar_tensor_tensor(
                        out=S[:, slot, j, :], in0=iota[:, :], scalar=rel_node[:, j:j + 1],
                        in1=ps[:, j * P:(j + 1) * P], op0=ALU.is_equal, op1=ALU.mult)
                return last

            def types(k):
                if layer == 0:
                    return nc.vector.tensor_tensor(
                        G0[:, k, :, D:GW], iota8[:, :].unsqueeze(1).to_broadcast([P, 4, R]),
                        typ_f[:, bass.ds((i * ring + k) * 4, 4)].unsqueeze(2).to_broadcast([P, 4, R]), ALU.is_equal)
                dve.wait_ge(rows_in[k % TYPE_RING], i * (16 * (ring // TYPE_RING)) + 16 * (k // TYPE_RING + 1))
                return nc.vector.tensor_scalar(TT[:, k % 2, :, :].rearrange("p j e -> p (j e)"),
                                               typ_rows[:, k % TYPE_RING, :], lane8[0:3 * R, :], None,
                                               ALU.is_equal).then_inc(sg["TT"], 1)

            def add(ps, t):
                rows = acc[:, bass.ds(t, 1), 0:width].rearrange("p a d -> p (a d)")
                return nc.vector.tensor_tensor(rows, rows, ps[:, 0:width], ALU.add)

            los = []
            types(0)
            for k in range(ring + 1):
                if k < ring:
                    g = i * ring + k
                    lo, hi = group_range(dve, g)
                    los.append(lo)
                    if k + 1 < ring:
                        types(k + 1)
                    one_hot(g, lo, k % 2, lambda: dve.wait_ge(sg["W"], i * ring + (k + 1)),
                            bank[3 + k % 2]).then_inc(sg["S"], 1)
                    with dve.If(hi > lo):
                        with dve.Fori(lo + 1, hi + 1) as t:
                            dve.reg_add(extra_dve, extra_dve, 1)
                            n = dve.snap(extra_dve, min_val=1, max_val=NG * NT)
                            dve.wait_ge(sg["mm"], g + 1).then_inc(s["dve_passed"], 1)
                            one_hot(g, t, k % 2, lambda: dve.wait_ge(sg["Wx"], n), bank[5]).then_inc(sg["Sx"], 1)
                            dve.drain()
                            dve.wait_ge(sg["mmx"], n)
                            add(bank[2], t)
                            dve.drain()
                if k >= 1:
                    dve.drain()
                    dve.wait_ge(sg["mm"], i * ring + k)
                    add(bank[(k - 1) % 2], los[k - 1]).then_inc(sg["added"], 1)

        def pe_turn(pe, layer, i):
            G, S, ring, sg = (G0, G1)[layer], (S0, S1)[layer], RINGS[layer], seg[layer]
            width = (GW, D)[layer]

            def inverse_counts(ps, t, slot):
                for j in range(4):
                    last = pe.matmul(ps[:, j * P:(j + 1) * P], TT[:, slot, j, :],
                                     invT[:, bass.ds(t * P, P)], start=True, stop=True)
                return last

            def product(ps, slot, k):
                for j in range(4):
                    last = pe.matmul(ps[:, 0:width], S[:, slot, j, :], G[:, k, j, 0:width],
                                     start=(j == 0), stop=(j == 3))
                return last

            ranges = []
            for k in range(-1, ring):
                if k + 1 < ring:
                    ranges.append(group_range(pe, i * ring + (k + 1)))
                    if layer == 1:
                        pe.wait_ge(sg["TT"], i * ring + (k + 2 + TYPE_RING))
                        inverse_counts(bank[3 + (k + 1) % 2], ranges[-1][0], (k + 1) % 2).then_inc(sg["W"], 1)
                if k < 0:
                    continue
                g = i * ring + k
                lo, hi = ranges[k]
                if layer == 1:
                    pe.wait_ge(gathered[1][k], i * 64 + 64)
                else:
                    pe.wait_ge(sg["scaled"], g + 1)
                pe.wait_ge(sg["S"], g + 1)
                pe.wait_ge(sg["added"], g + (ring - 1))
                product(bank[k % 2], k % 2, k).then_inc(sg["mm"], 1)
                with pe.If(hi > lo):
                    with pe.Fori(lo + 1, hi + 1) as t:
                        pe.reg_add(extra_pe, extra_pe, 1)
                        n = pe.snap(extra_pe, min_val=1, max_val=NG * NT)
                        if layer == 1:
                            inverse_counts(bank[5], t, k % 2).then_inc(sg["Wx"], 1)
                        pe.wait_ge(sg["Sx"], n)
                        product(bank[2], k % 2, k).then_inc(sg["mmx"], 1)

        def turns_of_step(eng, b, turn):
            done = eng.value_load(turns[0:1, bass.ds(b, 1)], min_val=0, max_val=TURNS)
            need = eng.value_load(turns[0:1, bass.ds(b + 1, 1)], min_val=0, max_val=TURNS)
            with eng.If(need > done):
                with eng.Fori(done, need) as i:
                    turn(i)

        def steps(eng, first, both, final):
            first(0)
            with eng.Fori(1, NB) as b:
                both(b)
            final(NB)

        extra_dve = nc.vector.alloc_register("extra_dve")
        extra_pe = nc.tensor.alloc_register("extra_pe")

        block = ctx.enter_context(nc.Block())

        @block.gpsimd
        def _(pool):
            g = nc.gpsimd
            g.memset(ident[:, :], 0.0).then_inc(s["consts"], 1)
            g.memset(ones[:, :], 1.0).then_inc(s["consts"], 1)
            g.memset(minus_half[:, :], -0.5).then_inc(s["consts"], 1)
            for t, step, num, base, lanes in ((iota, 1, P, 0, 0), (iota8, 1, R, 0, 0), (iota_rev, -1, R, R, 0),
                                              (tile_base, P, NT, 0, 0), (lane_i, 0, 1, 0, 1),
                                              (turn1, 1, TURNS, 1, 0), (bound, 2, NB, 1, 0)):
                g.iota(t[:, :], pattern=[[step, num]], base=base, channel_multiplier=lanes,
                       allow_small_or_imprecise_dtypes=True).then_inc(s["consts"], 1)
            pool.wait_ge(s["consts"], 10)
            g.affine_select(out=ident[:, :], in_=ident[:, :], compare_op=ALU.not_equal, fill=1.0, base=0,
                            pattern=[[-1, P]], channel_multiplier=1).then_inc(s["consts"], 1)
            pool.wait_ge(s["table0_stats"], 1)
            g.tensor_tensor(rstd[:, :], var_eps[:, :], minus_half[:, :], ALU.pow).then_inc(s["table0_rstd"], 1)
            pool.wait_ge(s["table0_out"], 16)
            pool_gather(pool, 0)
            pool.wait_ge(s["x1_stats"], 1)
            g.tensor_tensor(rstd[:, :], var_eps[:, :], minus_half[:, :], ALU.pow).then_inc(s["x1_rstd"], 1)
            with pool.Fori(0, NB) as b:
                for n, var, out_sem in ((0, s["ln1_var"], s["ln1_rstd"]), (1, s["ln2_var"], s["ln2_rstd"])):
                    pool.wait_ge(var, b + 1)
                    g.tensor_tensor(ln_rs[:, n, :], ln_ve[:, n, :], minus_half[:, 0:2], ALU.pow).then_inc(out_sem, 1)
            for r in range(4):
                pool.wait_ge(y_out[r], 16 * (NT + 1))
            pool_gather(pool, 1)

        @block.sync
        def _(sp):
            for r in range(4):
                sp.sem_inc(y_out[r], 16)
            sp.sem_inc(s["o_out"], 16)
            sp.dma_start(dst_rows[:, :, :], dst_flat.rearrange("(a r c) -> r a c", a=4, c=GE)).then_inc(s["range_in"], 16)
            sp.dma_start(X, tiles_of(x)).then_inc(s["x_in"], 16)
            sp.dma_start(src_i[:, :], src).then_inc(s["edges_in"], 16)
            sp.dma_start(dst_i, dst).then_inc(s["edges_in"], 16)
            sp.dma_start(typ_i, typ).then_inc(s["edges_in"], 16)
            sp.dma_start(w_e[:, :], wgt).then_inc(s["edges_in"], 16)
            sp.wait_ge(s["range_ready"], 1)
            sp.dma_start(range_dram.rearrange("(a r) c -> r a c", a=4), range_i[:, :, :]).then_inc(s["range_out"], 16)
            sp.wait_ge(s["range_out"], 16)
            sp.dma_start(tile_range[:, :], range_dram.rearrange("(a g) c -> a (g c)", a=1)).then_inc(s["range_in"], 16)
            sp.wait_ge(s["table0_normed"], 1)
            sp.dma_start(tiles_of(table0), acc[:, :, 0:D]).then_inc(s["table0_out"], 16)
            sp.wait_ge(seg[0]["added"], NG + RINGS[0])
            sp.dma_start(Wg[:, :, :], W_gnn0.rearrange("(k p) n -> p k n", p=P)).then_inc(s["update_in"], 16)
            sp.dma_start(Wr_sb[:, :, :], Wr.rearrange("(k p) n -> p k n", p=P)).then_inc(s["update_in"], 16)
            sp.dma_start(br_sb[:, :], br.rearrange("(a n) -> a n", a=1)).then_inc(s["update_in"], 16)
            sp.wait_ge(s["chosen_ready"], 1)
            for n in range(2):
                e = sp.value_load(chosen[0:1, n:n + 1], min_val=0, max_val=NE - 1)
                sp.dma_start(Wsel1[:, n, :, :], W1_0[bass.ds(e, 1), :, :].rearrange("a (k p) f -> p (a k) f", p=P)
                             ).then_inc(s["chosen_in"], 16)
                sp.dma_start(Wsel2[:, n, :, :], W2_0[bass.ds(e, 1), :, :].rearrange("a (k p) d -> p (a k) d", p=P)
                             ).then_inc(s["chosen_in"], 16)
                sp.dma_start(b1s[:, n, :], b1_0[bass.ds(e, 1), :, :].rearrange("a p k -> p (a k)")
                             ).then_inc(s["chosen_in"], 16)
                sp.dma_start(b2s[:, n, :], b2_0[bass.ds(e, 1), :]).then_inc(s["chosen_in"], 16)
            for t, v in ((gam, gamma), (bet, beta), (bias_b, bias1)):
                sp.dma_start(t[:, :], v.rearrange("(a n) -> a n", a=1).to_broadcast([P, D])).then_inc(s["middle_in"], 16)
            for r in range(R):
                sp.dma_start(Wrel[:, :, r * D:(r + 1) * D], W_rel[r].rearrange("(k p) n -> p k n", p=P)
                             ).then_inc(s["middle_in"], 16)
            sp.dma_start(Wrel[:, :, R * D:], W_root.rearrange("(k p) n -> p k n", p=P)).then_inc(s["middle_in"], 16)
            with sp.Fori(0, NB) as b:
                sp.wait_ge(s["x2_ready"], b + 1)
                sp.dma_start(tiles_of(x2_dram)[:, bass.ds(b * 2, 2), :], X[:, bass.ds(b * 2, 2), :]).then_inc(s["x2_out"], 16)
                for t in range(2):
                    for r in range(4):
                        sp.wait_ge(s["y_sb"], b * 8 + (4 * t + r + 3))
                        sp.dma_start(table1.rearrange("(t p r) d -> p t (r d)", p=P, r=R)
                                     [:, bass.ds(b * 2 + t, 1), r * 2 * D:(r + 1) * 2 * D].rearrange("p a d -> p (a d)"),
                                     Y[:, r, :]).then_inc(y_out[r], 16)
            sp.wait_ge(s["x2_out"], 16 * NB)
            sp.wait_ge(s["root_sb"], NT + 2)
            for e in range(NE):
                sp.dma_start(W1e[:, e, :, :], W1_1[e].rearrange("(k p) f -> p k f", p=P)).then_inc(s["experts_in"], 16)
                sp.dma_start(W2e[:, e, :, :], W2_1[e].rearrange("(k p) d -> p k d", p=P)).then_inc(s["experts_in"], 16)
            for r in range(4):
                sp.wait_ge(y_out[r], 16 * (NT + 1))
            sp.dma_start(gw[:, :, :], gate_w.rearrange("(k p) n -> p k n", p=P)).then_inc(s["last_in"], 16)
            sp.dma_start(gbb[:, :], gate_b.rearrange("(a n) -> a n", a=1).to_broadcast([P, NE])).then_inc(s["last_in"], 16)
            sp.dma_start(b1e[:, :, :], b1_1.rearrange("e p k -> p e k")).then_inc(s["last_in"], 16)
            sp.dma_start(b2e[:, :], b2_1).then_inc(s["last_in"], 16)

            def turn(i):
                for k in range(RINGS[1]):
                    g = i * RINGS[1] + k
                    sp.wait_ge(seg[1]["TT"], g + 1)
                    sp.dma_start(typ_rows[:, k % TYPE_RING, :], typ_flat.rearrange("(a g) -> a g", a=1)
                                 [:, bass.ds(g * GE, GE)].to_broadcast([3 * R, GE])).then_inc(rows_in[k % TYPE_RING], 16)

            def load_x2(b):
                sp.wait_ge(s["qT_ps"], b + 1)
                sp.dma_start(x2in[:, :, :], tiles_of(x2_dram)[:, bass.ds(b * 2, 2), :]).then_inc(s["x2_in"], 16)

            def store(b):
                sp.wait_ge(s["o_ready"], b + 1)
                sp.dma_start(tiles_of(out)[:, bass.ds(b * 2, 2), :], o[:, :, :]).then_inc(s["o_out"], 16)

            for b in range(2):
                turns_of_step(sp, b, turn)
                load_x2(b)
            with sp.Fori(2, NB) as b:
                turns_of_step(sp, b, turn)
                load_x2(b)
                store(b - 2)
            store(NB - 2)
            store(NB - 1)
            sp.wait_ge(s["o_out"], 16 * (NB + 1))

        @block.scalar
        def _(act):
            act.wait_ge(s["edges_in"], 64)
            act_first_rows(0)
            with act.Fori(0, NG // RINGS[0]) as i:
                act_turn(act, 0, i)
            act.wait_ge(seg[0]["added"], NG + RINGS[0])
            with act.Fori(0, NB) as b:
                act.wait_ge(s["aggT_ps"], b + 1)
                nc.scalar.copy(aggS[:, :, :], acc[:, bass.ds(b * 2, 2), 0:D]).then_inc(s["agg_copied"], 1)
            for c in range(7):
                act.wait_ge(s["invT_ps"], c + 1)
                n = min(8, NT - 8 * c)
                nc.scalar.copy(invT[:, 8 * c * P:(8 * c + n) * P], bank[4 + c % 2][0:3 * R, :].bitcast(BF16)[:, 0:n * P]
                               ).then_inc(s["invT_sb"], 1)
            for n in range(3):
                act.wait_ge(s["soft_in"], n + 1)
                w = NE if n < 2 else 1
                nc.scalar.activation(gt[:, 1, 0:w], gt[:, 0, 0:w], ACT.Exp).then_inc(s["soft_exp"], 1)
            act.wait_ge(s["row_sb"], 1)
            act.wait_ge(s["chosen_in"], 16 * 8)
            for n in range(2):
                nc.scalar.activation(Wsel2[:, n, :, :], Wsel2[:, n, :, :], ACT.Copy, scale=gate_b0[:, n:n + 1]
                                     ).then_inc(s["chosen_scaled"], 1)
            with act.Fori(0, NB) as b:
                act.wait_ge(s["h0T_ps"], b + 1)
                nc.scalar.copy(h0T[:, :, :].rearrange("p k t -> p (k t)"), bank[0][:, :]).then_inc(s["h0T_sb"], 1)
                for u in range(4):
                    act.wait_ge(s["f1_ps"], b * 4 + (u + 1))
                    for v in range(2):
                        n, f = divmod(2 * u + v, KF)
                        gelu = nc.scalar.activation(hT[:, n, f, :], bank[1 + u % 2][:, v * TOK:(v + 1) * TOK],
                                                    ACT.Gelu, bias=b1s[:, n, f:f + 1])
                    gelu.then_inc(s["f1_sb"], 1)
                act.wait_ge(s["hnT_ps"], b + 1)
                nc.scalar.copy(hnT[:, :, :].rearrange("p k t -> p (k t)"), bank[0][:, :]).then_inc(s["hnT_sb"], 1)
                for t in range(2):
                    for r in range(4):
                        act.wait_ge(y_out[r], b * 32 + (16 * t + 16))
                        act.wait_ge(s["y_ps"], b * 8 + (4 * t + r + 1))
                        nc.scalar.copy(Y[:, r, :], bank[4 + r % 2][:, :]).then_inc(s["y_sb"], 1)
            act_first_rows(1)
            act.wait_ge(s["last_in"], 64)

            def hidden(b, e):
                for u in range(2):
                    act.wait_ge(s["u1_ps"], b * (2 * NE) + (2 * e + u + 1))
                    for v in range(2):
                        f = 2 * u + v
                        gelu = nc.scalar.activation(qh[:, e % 2, f, :], bank[1 + u][:, v * TOK:(v + 1) * TOK],
                                                    ACT.Gelu, bias=b1e[:, e, f:f + 1])
                    gelu.then_inc(s["u1_sb"], 1)

            def spread(b):
                act.wait_ge(s["x3_var"], b + 1)
                nc.scalar.activation(sd[:, :], sd[:, :], ACT.Sqrt).then_inc(s["x3_sd"], 1)

            def transposed(b):
                act.wait_ge(s["qT_ps"], b + 2)
                nc.scalar.copy(qT[:, :, :].rearrange("p k t -> p (k t)"), bank[0][:, :]).then_inc(s["qT_sb"], 1)

            def step(b, sums=True, experts=True):
                if sums:
                    turns_of_step(act, b, lambda i: act_turn(act, 1, i))
                if experts:
                    hidden(b - 1, 0)
                    hidden(b - 1, 1)
                    act.wait_ge(s["exp_in"], b)
                    nc.scalar.activation(gs[:, 1, :, :], gs[:, 0, :, :], ACT.Exp).then_inc(s["exp_out"], 1)
                if sums:
                    spread(b)
                if experts:
                    for e in range(2, NE):
                        hidden(b - 1, e)
                if sums:
                    transposed(b)

            steps(act, lambda b: step(b, experts=False), step, lambda b: step(b, sums=False))

        @block.tensor
        def _(pe):
            pe.sem_inc(s["aggT_ps"], 1)
            pe.sem_inc(s["qT_ps"], 1)
            pe.wait_ge(s["consts2"], 1)
            pe.wait_ge(s["range_in"], 32)
            pe.reg_mov(extra_pe, 0)
            with pe.Fori(0, NG // RINGS[0]) as i:
                pe_turn(pe, 0, i)
            pe.wait_ge(s["update_in"], 48)

            def transposes(ps, tiles, count):
                for t in range(2):
                    for k in range(KD):
                        last = pe.transpose(ps[:, (2 * k + t) * P:(2 * k + t + 1) * P], tiles[:, t, k * P:(k + 1) * P],
                                            ident[:, :])
                return last.then_inc(count, 1)

            with pe.Fori(0, NB) as b:
                pe.wait_ge(s["agg_copied"], b + 1)
                transposes(bank[0], aggS, s["aggT_ps"])
                pe.wait_ge(s["aggT_sb"], b + 1)
                for t in range(2):
                    for k in range(KD):
                        mm = pe.matmul(bank[1][:, t * D:(t + 1) * D], aggT[:, k, t, :], Wg[:, k, :],
                                       start=(k == 0), stop=(k == KD - 1))
                mm.then_inc(s["agg_ps"], 1)
            pe.wait_ge(s["inv_ready"], 1)
            for c in range(7):
                if c >= 2:
                    pe.wait_ge(s["invT_sb"], c - 1)
                for t in range(8 * c, min(8 * c + 8, NT)):
                    tr = pe.transpose(bank[4 + c % 2][0:3 * R, :].bitcast(BF16)[:, (t % 8) * P:(t % 8 + 1) * P],
                                      inv3[:, t, :, :].rearrange("p a r -> p (a r)"), identb[:, :])
                tr.then_inc(s["invT_ps"], 1)
            pe.wait_ge(s["hsum_ready"], 1)
            for k in range(KD):
                mm = pe.matmul(bank[6][:, k:k + 1], hsum[:, k * P:(k + 1) * P], ones[:, 0:1], start=True, stop=True)
            mm.then_inc(s["mean_ps"], 1)
            pe.wait_ge(s["mean_sb"], 1)
            for k in range(KD):
                mm = pe.matmul(bank[7][0:1, 0:NE], mean_sb[:, k:k + 1], Wr_sb[:, k, :], start=(k == 0), stop=(k == KD - 1))
            mm.then_inc(s["logit_ps"], 1)
            pe.wait_ge(s["row_ready"], 1)
            pe.matmul(bank[6][:, 0:2 + D], ones[0:1, :], row[0:1, :], start=True, stop=True).then_inc(s["row_ps"], 1)
            pe.wait_ge(s["chosen_in"], 16 * 8)
            pe.wait_ge(s["middle_in"], 16 * (R + 4))
            pe.wait_ge(s["chosen_scaled"], 2)
            with pe.Fori(0, NB) as b:
                pe.wait_ge(s["h0_ready"], b + 1)
                transposes(bank[0], h0, s["h0T_ps"])
                pe.wait_ge(s["h0T_sb"], b + 1)
                for u in range(4):
                    if u >= 2:
                        pe.wait_ge(s["f1_sb"], b * 4 + (u - 1))
                    for v in range(2):
                        n, f = divmod(2 * u + v, KF)
                        for k in range(KD):
                            mm = pe.matmul(bank[1 + u % 2][:, v * TOK:(v + 1) * TOK],
                                           Wsel1[:, n, k, f * P:(f + 1) * P], h0T[:, k, :],
                                           start=(k == 0), stop=(k == KD - 1))
                    mm.then_inc(s["f1_ps"], 1)
                pe.wait_ge(s["f1_sb"], b * 4 + 4)
                for t in range(2):
                    for n in range(2):
                        for f in range(KF):
                            mm = pe.matmul(bank[3][:, t * D:(t + 1) * D], hT[:, n, f, t * P:(t + 1) * P],
                                           Wsel2[:, n, f, :], start=(n == 0 and f == 0), stop=(n == 1 and f == KF - 1))
                mm.then_inc(s["f2_ps"], 1)
                pe.wait_ge(s["hn_ready"], b + 1)
                transposes(bank[0], hn, s["hnT_ps"])
                pe.wait_ge(s["hnT_sb"], b + 1)
                for t in range(2):
                    for r in range(4):
                        pe.wait_ge(s["y_sb"], b * 8 + (4 * t + r + 1))
                        for k in range(KD):
                            mm = pe.matmul(bank[4 + r % 2][:, :], hnT[:, k, t * P:(t + 1) * P],
                                           Wrel[:, k, r * 2 * D:(r + 1) * 2 * D], start=(k == 0), stop=(k == KD - 1))
                        mm.then_inc(s["y_ps"], 1)
                    pe.wait_ge(s["root_sb"], b * 2 + (t + 1))
                    for k in range(KD):
                        mm = pe.matmul(bank[6 + t][:, 0:D], hnT[:, k, t * P:(t + 1) * P], Wrel[:, k, R * D:],
                                       start=(k == 0), stop=(k == KD - 1))
                    mm.then_inc(s["root_ps"], 1)
            pe.reg_mov(extra_pe, 0)
            pe.wait_ge(s["last_in"], 64)
            pe.wait_ge(s["experts_in"], 16 * 2 * NE)

            def hidden(b, e):
                for u in range(2):
                    pe.wait_ge(s["u1_sb"], b * (2 * NE) + (2 * e + u + 1))
                    for v in range(2):
                        f = 2 * u + v
                        for k in range(KD):
                            mm = pe.matmul(bank[1 + u][:, v * TOK:(v + 1) * TOK], W1e[:, e, k, f * P:(f + 1) * P],
                                           qT[:, k, :], start=(k == 0), stop=(k == KD - 1))
                    mm.then_inc(s["u1_ps"], 1)

            def output(b, e):
                pe.wait_ge(s["u1_sb"], b * (2 * NE) + (2 * e + 4))
                pe.wait_ge(s["u2_sb"], b * NE + (e + 1))
                for t in range(2):
                    for f in range(KF):
                        mm = pe.matmul(bank[3 + e % 2][:, t * D:(t + 1) * D], qh[:, e % 2, f, t * P:(t + 1) * P],
                                       W2e[:, e, f, :], start=(f == 0), stop=(f == KF - 1))
                mm.then_inc(s["u2_ps"], 1)

            def gated_biases(b):
                pe.wait_ge(s["cw_ready"], b + 1)
                for t in range(2):
                    tr = pe.transpose(bank[7][0:NE, t * P:(t + 1) * P], cwS[:, t, :], ident[:, :])
                tr.then_inc(s["cwT_ps"], 1)
                pe.wait_ge(s["cwT_sb"], b + 1)
                for t in range(2):
                    mm = pe.matmul(bank[6][:, t * D:(t + 1) * D], cwT[:, t, :], b2e[:, :], start=True, stop=True)
                mm.then_inc(s["bias_ps"], 1)

            def logit_products(b):
                pe.wait_ge(s["q_ready"], b + 1)
                transposes(bank[0], q, s["qT_ps"])
                pe.wait_ge(s["qT_sb"], b + 1)
                for t in range(2):
                    for k in range(KD):
                        mm = pe.matmul(bank[7][:, 2 * P + t * NE:2 * P + (t + 1) * NE], qT[:, k, t * P:(t + 1) * P],
                                       gw[:, k, :], start=(k == 0), stop=(k == KD - 1))
                mm.then_inc(s["lg_ps"], 1)

            def step(b, sums=True, experts=True):
                if sums:
                    turns_of_step(pe, b, lambda i: pe_turn(pe, 1, i))
                    summed = pe.value_load(turns[0:1, bass.ds(b + 1, 1)], min_val=0, max_val=TURNS) * RINGS[1]
                else:
                    summed = NG
                if experts:
                    pe.wait_ge(seg[1]["added"], summed + RINGS[1])
                    for e in range(NE + 1):
                        if e < NE:
                            hidden(b - 1, e)
                        if e == 1:
                            gated_biases(b - 1)
                        if e >= 1:
                            output(b - 1, e - 1)
                if sums:
                    logit_products(b)

            steps(pe, lambda b: step(b, experts=False), step, lambda b: step(b, sums=False))

        @block.vector
        def _(dve):
            v = nc.vector
            dve.drain().then_inc(s["y_sb"], 2)
            dve.drain().then_inc(s["root_sb"], 2)
            dve.drain().then_inc(s["u1_sb"], 2)
            dve.drain().then_inc(s["u2_sb"], 2)

            def row_stats(rows, b):
                for t in range(2):
                    v.bn_stats(stats[:, t, :], rows[:, bass.ds(b * 2 + t, 1), 0:D].rearrange("p a d -> p (a d)"))
                dve.drain()
                for t in range(2):
                    v.bn_aggr(mv2[:, t, :], stats[:, t, :])
                dve.drain()
                v.tensor_copy(mv[:, bass.ds(b * 2, 2), :], mv2[:, :, :])

            dve.wait_ge(s["consts"], 11)
            v.tensor_copy(identb[:, :], ident[:, :])
            v.tensor_scalar(lane8_i[:, :], lane_i[:, :], R - 1, None, ALU.bitwise_and)
            dve.drain()
            v.tensor_copy(lane8[:, :], lane8_i[:, :]).then_inc(s["consts2"], 1)
            dve.wait_ge(s["range_in"], 16)
            v.tensor_reduce(range_n[:, :, 0:1], dst_rows[:, :, :], AX.X, ALU.min)
            v.tensor_reduce(range_n[:, :, 1:2], dst_rows[:, :, :], AX.X, ALU.max)
            dve.drain()
            v.tensor_scalar(range_i[:, :, :], range_n[:, :, :], 7, None, ALU.arith_shift_right).then_inc(s["range_ready"], 1)
            dve.wait_ge(s["x_in"], 16)
            with dve.Fori(0, NB) as b:
                row_stats(X, b)
            dve.drain()
            v.tensor_scalar(var_eps[:, :], mv[:, :, 1], EPS, None, ALU.add).then_inc(s["table0_stats"], 1)
            dve.wait_ge(s["table0_rstd"], 1)
            with dve.Fori(0, NT) as t:
                v.tensor_scalar(acc[:, bass.ds(t, 1), 0:D].rearrange("p a d -> p (a d)"),
                                X[:, bass.ds(t, 1), :].rearrange("p a d -> p (a d)"),
                                mv[:, bass.ds(t, 1), 0:1].rearrange("p a d -> p (a d)"), rstd[:, bass.ds(t, 1)],
                                ALU.subtract, ALU.mult)
            dve.drain().then_inc(s["table0_normed"], 1)
            dve.wait_ge(s["edges_in"], 64)
            v.tensor_copy(dst_f[:, :], dst_i)
            v.tensor_copy(typ_f[:, :], typ_i)
            v.memset(idx1[:, NG * 4:], 0)
            v.scalar_tensor_tensor(out=idx1[:, 0:NG * 4], in0=src_i[:, 0:NG * 4], scalar=float(R), in1=typ_i,
                                   op0=ALU.mult, op1=ALU.add)
            dve.wait_ge(s["table0_out"], 16)
            v.memset(acc[:, :, :], 0.0)
            dve.wait_ge(s["range_in"], 32)
            v.tensor_reduce(turn_lo[:, :], tile_range[:, :].rearrange("a (i k c) -> a i c k", k=RINGS[1], c=2)[:, :, 0, :],
                            AX.X, ALU.min)
            dve.drain()
            v.tensor_tensor(turn_of[:, :, :], turn_lo[:, :].unsqueeze(1).to_broadcast([1, NB, TURNS]),
                            bound[:, :].unsqueeze(2).to_broadcast([1, NB, TURNS]), ALU.is_le)
            dve.drain()
            v.tensor_tensor(turn_of[:, :, :], turn_of[:, :, :], turn1[:, :].unsqueeze(1).to_broadcast([1, NB, TURNS]),
                            ALU.mult)
            dve.drain()
            v.tensor_reduce(turns_f[:, :], turn_of[:, :, :], AX.X, ALU.max)
            v.memset(turns[:, 0:1], 0)
            dve.drain()
            v.tensor_copy(turns[:, 1:], turns_f[:, :])
            dve.drain().then_inc(seg[0]["added"], RINGS[0])
            dve.reg_mov(extra_dve, 0)
            with dve.Fori(0, NG // RINGS[0]) as i:
                dve_turn(dve, 0, i)

            with dve.Fori(0, NB) as b:
                dve.wait_ge(s["aggT_ps"], b + 2)
                v.tensor_copy(aggT[:, :, :, :].rearrange("p k t c -> p (k t c)"), bank[0][:, :]).then_inc(s["aggT_sb"], 1)
                dve.wait_ge(s["agg_ps"], b + 1)
                v.tensor_tensor(X[:, bass.ds(b * 2, 2), :], X[:, bass.ds(b * 2, 2), :],
                                bank[1][:, :].rearrange("p (t d) -> p t d", t=2), ALU.add)
                dve.drain()
                row_stats(X, b)
            dve.drain()
            v.tensor_scalar(var_eps[:, :], mv[:, :, 1], EPS, None, ALU.add).then_inc(s["x1_stats"], 1)
            v.tensor_scalar(inv[:, :, :], acc[:, :, D:GW], 1.0, None, ALU.max)
            dve.drain()
            v.reciprocal(inv[:, :, :], inv[:, :, :])
            for part in range(3):
                dve.drain()
                v.tensor_copy(inv3[:, :, part, :], inv[:, :, :])
                if part < 2:
                    dve.drain()
                    v.tensor_tensor(inv[:, :, :], inv[:, :, :], inv3[:, :, part, :], ALU.subtract)
            dve.drain().then_inc(s["inv_ready"], 1)
            dve.wait_ge(s["x1_rstd"], 1)
            v.tensor_tensor(rm[:, :], rstd[:, :], mv[:, :, 0], ALU.mult)
            v.memset(hsum[:, :], 0.0)
            dve.drain()
            v.tensor_reduce(rm_sum[:, :], rm[:, :], AX.X, ALU.add)
            with dve.Fori(0, NT) as t:
                dve.drain()
                v.scalar_tensor_tensor(out=hsum[:, :], in0=X[:, bass.ds(t, 1), :].rearrange("p a d -> p (a d)"),
                                       scalar=rstd[:, bass.ds(t, 1)], in1=hsum[:, :], op0=ALU.mult, op1=ALU.add)
            dve.drain()
            v.tensor_scalar(hsum[:, :], hsum[:, :], rm_sum[:, :], None, ALU.subtract).then_inc(s["hsum_ready"], 1)
            dve.wait_ge(s["mean_ps"], 1)
            v.tensor_scalar(mean_sb[:, :], bank[6][:, 0:KD], 1.0 / N, None, ALU.mult).then_inc(s["mean_sb"], 1)

            def softmax(src_row, n):
                v.tensor_reduce(gc[:, 0:1], src_row, AX.X, ALU.max)
                dve.drain()
                v.tensor_scalar(gt[:, 0, :], src_row, gc[:, 0:1], None, ALU.subtract).then_inc(s["soft_in"], 1)
                dve.wait_ge(s["soft_exp"], n)
                v.tensor_reduce(gc[:, 1:2], gt[:, 1, :], AX.X, ALU.add)
                dve.drain()
                v.reciprocal(gc[:, 2:3], gc[:, 1:2])
                dve.drain()
                v.tensor_scalar(gt[:, 3, :], gt[:, 1, :], gc[:, 2:3], None, ALU.mult)
                dve.drain()

            dve.wait_ge(s["logit_ps"], 1)
            v.tensor_tensor(gt[:, 2, :], bank[7][0:1, 0:NE], br_sb[:, :], ALU.add)
            dve.drain()
            softmax(gt[:, 2, :], 1)
            v.tensor_scalar(gt[:, 4, :], gt[:, 3, :], float(N), CAPACITY, ALU.mult, ALU.max)
            dve.drain()
            v.reciprocal(gt[:, 5, :], gt[:, 4, :])
            dve.drain()
            v.scalar_tensor_tensor(out=gt[:, 6, :], in0=gt[:, 5, :], scalar=CAPACITY, in1=gt[:, 3, :],
                                   op0=ALU.mult, op1=ALU.mult)
            dve.drain()
            softmax(gt[:, 6, :], 2)
            v.tensor_copy(gt[:, 4, :], gt[:, 3, :])
            dve.drain()
            for n in range(2):
                v.tensor_reduce(gc[:, 4 + n:5 + n], gt[:, 4, :], AX.X, ALU.max)
                dve.drain()
                v.scalar_tensor_tensor(out=gt[:, 7, :], in0=gt[:, 4, :], scalar=gc[:, 4 + n:5 + n],
                                       in1=iota_rev[0:1, :], op0=ALU.is_equal, op1=ALU.mult)
                dve.drain()
                v.tensor_reduce(gc[:, 6 + n:7 + n], gt[:, 7, :], AX.X, ALU.max)
                dve.drain()
                v.tensor_scalar(gt[:, 8, :], gt[:, 7, :], gc[:, 6 + n:7 + n], None, ALU.is_equal)
                dve.drain()
                v.scalar_tensor_tensor(out=gt[:, 4, :], in0=gt[:, 8, :], scalar=-4.0, in1=gt[:, 4, :],
                                       op0=ALU.mult, op1=ALU.add)
                dve.drain()
            v.tensor_tensor(gt[:, 0, 0:1], gc[:, 5:6], gc[:, 4:5], ALU.subtract).then_inc(s["soft_in"], 1)
            dve.wait_ge(s["soft_exp"], 3)
            v.tensor_scalar(gc[:, 8:9], gt[:, 1, 0:1], 1.0, None, ALU.add)
            dve.drain()
            v.reciprocal(gc[:, 9:10], gc[:, 8:9])
            dve.drain()
            v.tensor_tensor(gc[:, 10:11], gc[:, 9:10], gt[:, 1, 0:1], ALU.mult)
            dve.wait_ge(s["invT_sb"], 7)
            dve.drain()
            v.tensor_copy(gates[:, :], gc[:, 9:11])
            v.tensor_scalar(chosen[:, :], gc[:, 6:8], -1.0, float(NE), ALU.mult, ALU.add).then_inc(s["chosen_ready"], 1)
            dve.wait_ge(s["chosen_in"], 16 * 8)
            dve.drain()
            v.tensor_copy(row[:, 0:2], gates[:, :])
            v.tensor_scalar(row[:, 2:], b2s[:, 0, :], gates[:, 0:1], None, ALU.mult)
            dve.drain()
            v.scalar_tensor_tensor(out=row[:, 2:], in0=b2s[:, 1, :], scalar=gates[:, 1:2], in1=row[:, 2:],
                                   op0=ALU.mult, op1=ALU.add)
            dve.drain().then_inc(s["row_ready"], 1)
            dve.wait_ge(s["row_ps"], 1)
            v.tensor_copy(gate_b0[:, :], bank[6][:, 0:2])
            v.tensor_copy(b2g[:, :], bank[6][:, 2:2 + D])
            dve.drain().then_inc(s["row_sb"], 1)
            dve.wait_ge(s["middle_in"], 16 * (R + 4))

            def per_tile(t):
                return t[:, :].unsqueeze(1).to_broadcast([P, 2, D])

            with dve.Fori(0, NB) as b:
                batch = bass.ds(b * 2, 2)
                for t in range(2):
                    v.tensor_scalar(h0[:, t, :], X[:, bass.ds(b * 2 + t, 1), :].rearrange("p a d -> p (a d)"),
                                    mv[:, bass.ds(b * 2 + t, 1), 0:1].rearrange("p a d -> p (a d)"),
                                    rstd[:, bass.ds(b * 2 + t, 1)], ALU.subtract, ALU.mult)
                dve.drain().then_inc(s["h0_ready"], 1)
                dve.wait_ge(s["f2_ps"], b + 1)
                v.tensor_tensor(z[:, :, :], bank[3][:, :].rearrange("p (t d) -> p t d", t=2), h0[:, :, :], ALU.add)
                dve.drain()
                v.tensor_tensor(z[:, :, :], z[:, :, :], per_tile(b2g), ALU.add)
                dve.drain()
                for n, tile, var, rs in ((0, z, s["ln1_var"], s["ln1_rstd"]), (1, None, s["ln2_var"], s["ln2_rstd"])):
                    for t in range(2):
                        a = z[:, t, :] if n == 0 else X[:, bass.ds(b * 2 + t, 1), :].rearrange("p a d -> p (a d)")
                        v.bn_stats(stats[:, t, :], a)
                    dve.drain()
                    for t in range(2):
                        v.bn_aggr(ln_mv[:, n, t, :], stats[:, t, :])
                    dve.drain()
                    v.tensor_scalar(ln_ve[:, n, :], ln_mv[:, n, :, 1], EPS, None, ALU.add).then_inc(var, 1)
                    dve.wait_ge(rs, b + 1)
                    for t in range(2):
                        a = z[:, t, :] if n == 0 else X[:, bass.ds(b * 2 + t, 1), :].rearrange("p a d -> p (a d)")
                        v.tensor_scalar((z if n == 0 else hn)[:, t, :], a, ln_mv[:, n, t, 0:1], ln_rs[:, n, t:t + 1],
                                        ALU.subtract, ALU.mult)
                    dve.drain()
                    if n == 0:
                        v.tensor_tensor(z[:, :, :], z[:, :, :], per_tile(gam), ALU.mult)
                        dve.drain()
                        v.tensor_tensor(z[:, :, :], z[:, :, :], per_tile(bet), ALU.add)
                        dve.drain()
                        v.tensor_tensor(X[:, batch, :], X[:, batch, :], z[:, :, :], ALU.add)
                        dve.drain().then_inc(s["x2_ready"], 1)
                dve.drain().then_inc(s["hn_ready"], 1)
                for t in range(2):
                    dve.wait_ge(s["root_ps"], b * 2 + (t + 1))
                    v.tensor_tensor(acc[:, bass.ds(b * 2 + t, 1), 0:D].rearrange("p a d -> p (a d)"), bank[6 + t][:, 0:D],
                                    bias_b[:, :], ALU.add).then_inc(s["root_sb"], 1)
            for r in range(4):
                dve.wait_ge(y_out[r], 16 * (NT + 1))
            dve.drain().then_inc(seg[1]["added"], RINGS[1])
            dve.drain().then_inc(seg[1]["TT"], TYPE_RING)
            dve.reg_mov(extra_dve, 0)
            dve.wait_ge(s["last_in"], 64)

            def over_experts(col):
                return col.unsqueeze(2).to_broadcast([P, 2, NE])

            rev = iota_rev[:, :].unsqueeze(1).to_broadcast([P, 2, NE])

            def make_gates(b):
                dve.drain()
                dve.wait_ge(s["lg_ps"], b + 1)
                v.tensor_tensor(logits[:, :, :], bank[7][:, 2 * P:2 * P + 2 * NE].rearrange("p (t e) -> p t e", t=2),
                                gbb[:, :].unsqueeze(1).to_broadcast([P, 2, NE]), ALU.add)
                dve.drain()
                v.tensor_reduce(gcol[:, 0, :], logits[:, :, :], AX.X, ALU.max)
                dve.drain()
                v.tensor_tensor(gs[:, 0, :, :], logits[:, :, :], over_experts(gcol[:, 0, :]), ALU.subtract
                                ).then_inc(s["exp_in"], 1)
                dve.wait_ge(s["exp_out"], b + 1)
                v.tensor_reduce(gcol[:, 0, :], gs[:, 1, :, :], AX.X, ALU.add)
                dve.drain()
                v.reciprocal(gcol[:, 1, :], gcol[:, 0, :])
                dve.drain()
                v.tensor_tensor(gs[:, 0, :, :], gs[:, 1, :, :], over_experts(gcol[:, 1, :]), ALU.mult)
                dve.drain()
                v.tensor_copy(gs[:, 1, :, :], gs[:, 0, :, :])
                for n in range(2):
                    dve.drain()
                    v.tensor_reduce(gcol[:, 0, :], gs[:, 1, :, :], AX.X, ALU.max)
                    dve.drain()
                    v.tensor_tensor(gs[:, 2, :, :], gs[:, 1, :, :], over_experts(gcol[:, 0, :]), ALU.is_equal)
                    dve.drain()
                    v.tensor_tensor(gs[:, 2, :, :], gs[:, 2, :, :], rev, ALU.mult)
                    dve.drain()
                    v.tensor_reduce(gcol[:, 1, :], gs[:, 2, :, :], AX.X, ALU.max)
                    dve.drain()
                    v.tensor_tensor(gs[:, 3 + n, :, :], gs[:, 2, :, :], over_experts(gcol[:, 1, :]), ALU.is_equal)
                    dve.drain()
                    v.scalar_tensor_tensor(out=gs[:, 1, :, :], in0=gs[:, 3 + n, :, :], scalar=-4.0, in1=gs[:, 1, :, :],
                                           op0=ALU.mult, op1=ALU.add)
                v.tensor_tensor(gs[:, 3, :, :], gs[:, 3, :, :], gs[:, 4, :, :], ALU.add)
                dve.drain()
                v.tensor_tensor(cwS[:, :, :], gs[:, 3, :, :], gs[:, 0, :, :], ALU.mult).then_inc(s["cw_ready"], 1)

            def norm(b):
                batch = bass.ds(b * 2, 2)
                dve.drain()
                dve.wait_ge(s["x2_in"], b * 16 + 16)
                v.scalar_tensor_tensor(out=acc[:, batch, 0:D], in0=acc[:, batch, 0:D], scalar=0.0, in1=x2in[:, :, :],
                                       op0=ALU.max, op1=ALU.add)
                dve.drain()
                for t in range(2):
                    v.bn_stats(stats[:, t, :], acc[:, bass.ds(b * 2 + t, 1), 0:D].rearrange("p a d -> p (a d)"))
                dve.drain()
                for t in range(2):
                    v.bn_aggr(mv3[:, t, :], stats[:, t, :])
                dve.drain()
                v.tensor_scalar(sd[:, :], mv3[:, :, 1], EPS, None, ALU.add).then_inc(s["x3_var"], 1)
                dve.wait_ge(s["x3_sd"], b + 1)
                v.reciprocal(rs3[:, :], sd[:, :])
                dve.drain()
                for t in range(2):
                    v.tensor_scalar(q[:, t, :], acc[:, bass.ds(b * 2 + t, 1), 0:D].rearrange("p a d -> p (a d)"),
                                    mv3[:, t, 0:1], rs3[:, t:t + 1], ALU.subtract, ALU.mult)
                dve.drain().then_inc(s["q_ready"], 1)

            def experts_sum(b):
                dve.wait_ge(s["cwT_ps"], b + 1)
                v.tensor_copy(cwT[:, :, :], bank[7][0:NE, 0:2 * P].rearrange("p (t c) -> p t c", t=2)
                              ).then_inc(s["cwT_sb"], 1)
                dve.drain()
                dve.wait_ge(s["bias_ps"], b + 1)
                dve.wait_ge(s["o_out"], b * 16 + 16)
                v.tensor_tensor(o[:, :, :], acc[:, bass.ds(b * 2, 2), 0:D],
                                bank[6][:, :].rearrange("p (t d) -> p t d", t=2), ALU.add)
                for e in range(NE):
                    dve.drain()
                    dve.wait_ge(s["u2_ps"], b * NE + (e + 1))
                    for t in range(2):
                        fma = v.scalar_tensor_tensor(out=o[:, t, :], in0=bank[3 + e % 2][:, t * D:(t + 1) * D],
                                                     scalar=cwS[:, t, e:e + 1], in1=o[:, t, :],
                                                     op0=ALU.mult, op1=ALU.add)
                    fma.then_inc(s["u2_sb"], 1)
                dve.drain().then_inc(s["o_ready"], 1)

            def step(b, sums=True, experts=True):
                if sums:
                    turns_of_step(dve, b, lambda i: dve_turn(dve, 1, i))
                if experts:
                    make_gates(b - 1)
                if sums:
                    norm(b)
                if experts:
                    experts_sum(b - 1)

            steps(dve, lambda b: step(b, experts=False), step, lambda b: step(b, sums=False))


def kernel(**inputs):
    import numpy as _np
    import concourse.bacc as _bacc
    from concourse import mybir as _mybir
    from concourse.bass_utils import run_bass_kernel_spmd as _run

    a = {k: _np.ascontiguousarray(v) for k, v in inputs.items()}
    pad = NG * GE - EDGES

    def padded(v, value, more=0):
        return _np.concatenate([v, _np.full(pad + more, value, v.dtype)])

    def by_partition(v):
        return _np.ascontiguousarray(v.reshape(-1, P).T)

    def hidden_bias(v):
        return _np.ascontiguousarray(v.reshape(NE, KF, P).transpose(0, 2, 1))

    dst_flat = padded(a["dst"], PAD_NODE)
    typ_flat = padded(a["edge_type_8"], 0)
    ins = {
        "x": _np.concatenate([a["x"], _np.zeros((NP - N, D), a["x"].dtype)]),
        "src": by_partition(padded(a["src"], 0, RINGS[0] * GE)),
        "dst": by_partition(dst_flat),
        "typ": by_partition(typ_flat),
        "wgt": by_partition(padded(a["edge_weight"], 0)),
        "dst_flat": dst_flat,
        "typ_flat": typ_flat,
        "W_gnn0": a["L0_gnn_weight"],
        "Wr": a["L0_ffn_Wr"],
        "br": a["L0_ffn_br"],
        "W1_0": a["L0_ffn_W1"],
        "b1_0": hidden_bias(a["L0_ffn_b1"]),
        "W2_0": a["L0_ffn_W2"],
        "b2_0": a["L0_ffn_b2"],
        "gamma": a["L0_ffn_gamma"],
        "beta": a["L0_ffn_beta"],
        "W_rel": a["L1_gnn_W"],
        "W_root": a["L1_gnn_W_root"],
        "bias1": a["L1_gnn_bias"],
        "gate_w": a["L1_ffn_gate_w"],
        "gate_b": a["L1_ffn_gate_b"],
        "W1_1": a["L1_ffn_W1"],
        "b1_1": hidden_bias(a["L1_ffn_b1"]),
        "W2_1": a["L1_ffn_W2"],
        "b2_1": a["L1_ffn_b2"],
    }
    nc = _bacc.Bacc("TRN2", target_bir_lowering=False, num_devices=1)
    arrays, args = {}, []
    for name, v in ins.items():
        arrays[f"in_{name}"] = v
        args.append(nc.dram_tensor(f"in_{name}", v.shape, _mybir.dt.from_np(v.dtype), kind="ExternalInput").ap())
    out = nc.dram_tensor("out_0_dram", (NP, D), _mybir.dt.float32, kind="ExternalOutput").ap()
    gnn_ffn_two_layers(nc, *args, out)
    r = _run(nc, [arrays], core_ids=[0])
    return r.results[0]["out_0_dram"][:N]
```

```python
from contextlib import ExitStack

import concourse.bass as bass
from concourse import mybir

P = 128
N = 6250
D = 256
KD = D // P
NT = 50
NP = NT * P
NB = NT // 2
TOK = 2 * P
EDGES = 200000
GE = 4 * P
NG = 392
RINGS = (8, 8)
TURNS = NG // RINGS[1]
TYPE_RING = 2
R = 8
NE = 8
F = 512
KF = F // P
GW = D + R
EPS = 1e-5
PAD_NODE = N
CAPACITY = float(-(-N * 5 // (4 * NE)))

ALU = mybir.AluOpType
ACT = mybir.ActivationFunctionType
AX = mybir.AxisListType
F32 = mybir.dt.float32
BF16 = mybir.dt.bfloat16
I32 = mybir.dt.int32


def gnn_ffn_two_layers(nc, x, src, dst, typ, wgt, dst_flat, typ_flat, W_gnn0, Wr, br, W1_0, b1_0, W2_0, b2_0,
                       gamma, beta, W_rel, W_root, bias1, gate_w, gate_b, W1_1, b1_1, W2_1, b2_1, out):
    table0 = nc.dram_tensor("table0", (NP, D), F32, kind="Internal").ap()
    table1 = nc.dram_tensor("table1", (NP * R, D), F32, kind="Internal").ap()
    x2_dram = nc.dram_tensor("x2_dram", (NP, D), F32, kind="Internal").ap()
    range_dram = nc.dram_tensor("range_dram", (NG, 2), I32, kind="Internal").ap()

    def tiles_of(t):
        return t.rearrange("(t p) d -> p t d", p=P)

    ctx = ExitStack()
    with ctx:
        def sem(name):
            return ctx.enter_context(nc.semaphore(name))

        def sb(name, shape, dt=F32, scope=ctx):
            return scope.enter_context(nc.sbuf_tensor(name, shape, dt))

        wx = sb("wx", [P, 2 * NE * KD * F])
        X = wx[:, 0:NT * D].rearrange("p (t d) -> p t d", t=NT)
        spare = wx[:, NT * D:]
        typ_i = spare[:, 0:NG * 4].bitcast(I32)
        dst_i = spare[:, NG * 4:2 * NG * 4].bitcast(I32)
        hsum = spare[:, 2 * NG * 4:2 * NG * 4 + D]
        Wsel1 = spare[:, 0:2 * KD * F].rearrange("p (s k f) -> p s k f", s=2, k=KD)
        W1e = wx[:, 0:NE * KD * F].rearrange("p (e k f) -> p e k f", e=NE, k=KD)
        W2e = wx[:, NE * KD * F:].rearrange("p (e k d) -> p e k d", e=NE, k=KF)
        acc = sb("acc", [P, NT, GW])
        dst_f = sb("dst_f", [P, NG * 4])
        idx1 = sb("idx1", [P, (NG + RINGS[1]) * 4], I32)
        invT = sb("invT", [3 * R, NP], BF16)
        tile_range = sb("tile_range", [1, NG * 2], I32)
        ident = sb("ident", [P, P])
        identb = sb("identb", [P, P], BF16)
        iota = sb("iota", [P, P])
        iota8 = sb("iota8", [P, R])
        iota_rev = sb("iota_rev", [P, R])
        lane_i = sb("lane_i", [P, 1], I32)
        lane8_i = sb("lane8_i", [P, 1], I32)
        lane8 = sb("lane8", [P, 1])
        tile_base = sb("tile_base", [P, NT])
        ones = sb("ones", [P, P])
        minus_half = sb("minus_half", [P, NT])
        stats = sb("stats", [P, 2, 6])
        mv = sb("mv", [P, NT, 2])
        var_eps = sb("var_eps", [P, NT])
        rstd = sb("rstd", [P, NT])
        rel_node = sb("rel_node", [P, 4])
        idx_slot = sb("idx_slot", [P, RINGS[1], 4], I32)
        turn1 = sb("turn1", [1, TURNS])
        bound = sb("bound", [1, NB])
        turn_lo = sb("turn_lo", [1, TURNS])
        turns_f = sb("turns_f", [1, NB])
        turns = sb("turns", [1, NB + 1], I32)
        chosen = sb("chosen", [1, 2], I32)
        gates = sb("gates", [1, 2])
        mv2 = sb("mv2", [P, 2, 2])
        var_sd = sb("var_sd", [P, 2])

        with ExitStack() as edges0:
            G0 = sb("G0", [P, RINGS[0], 4, GW], F32, edges0)
            S0 = sb("S0", [P, 2, 4, P], F32, edges0)
            src_i = sb("src_i", [P, (NG + RINGS[0]) * 4], I32, edges0)
            typ_f = dst_i.bitcast(F32)
            w_e = sb("w_e", [P, NG * 4], F32, edges0)
            first_use = G0[:, :, :, :].rearrange("p k j c -> p (k j c)")
            dst_rows = first_use[0:98, 0:4 * GE].bitcast(I32).rearrange("p (a c) -> p a c", a=4)
            turn_of = first_use[0:1, 0:NB * TURNS].rearrange("p (b i) -> p b i", b=NB)
            range_n = sb("range_n", [98, 4, 2], I32, edges0)
            range_i = sb("range_i", [98, 4, 2], I32, edges0)
            Wg = sb("Wg", [P, KD, D], F32, edges0)
            aggS = sb("aggS", [P, 2, D], F32, edges0)
            aggT = sb("aggT", [P, KD, 2, P], F32, edges0)
        with ExitStack() as update0:
            inv = sb("inv", [P, NT, R], F32, update0)
            inv3 = sb("inv3", [P, NT, 3, R], BF16, update0)
            rm = sb("rm", [P, NT], F32, update0)
            rm_sum = sb("rm_sum", [P, 1], F32, update0)
            Wr_sb = sb("Wr_sb", [P, KD, NE], F32, update0)
            br_sb = sb("br_sb", [1, NE], F32, update0)
            mean_sb = sb("mean_sb", [P, KD], F32, update0)
            gt = sb("gt", [1, 12, NE], F32, update0)
            gc = sb("gc", [1, 12], F32, update0)
        with ExitStack() as middle:
            Wrel = sb("Wrel", [P, KD, (R + 1) * D], F32, middle)
            Wsel2 = sb("Wsel2", [P, 2, KF, D], F32, middle)
            gate_b0 = sb("gate_b0", [P, 2], F32, middle)
            b1s = sb("b1s", [P, 2, KF], F32, middle)
            b2s = sb("b2s", [1, 2, D], F32, middle)
            row = sb("row", [1, 2 + D], F32, middle)
            b2g = sb("b2g", [P, D], F32, middle)
            gam = sb("gam", [P, D], F32, middle)
            bet = sb("bet", [P, D], F32, middle)
            bias_b = sb("bias_b", [P, D], F32, middle)
            h0 = sb("h0", [P, 2, D], F32, middle)
            h0T = sb("h0T", [P, KD, TOK], F32, middle)
            hT = sb("hT", [P, 2, KF, TOK], F32, middle)
            z = sb("z", [P, 2, D], F32, middle)
            hn = sb("hn", [P, 2, D], F32, middle)
            hnT = sb("hnT", [P, KD, TOK], F32, middle)
            Y = sb("Y", [P, 4, 2 * D], F32, middle)
            ln_mv = sb("ln_mv", [P, 2, 2, 2], F32, middle)
            ln_ve = sb("ln_ve", [P, 2, 2], F32, middle)
            ln_rs = sb("ln_rs", [P, 2, 2], F32, middle)
        with ExitStack() as last:
            G1 = sb("G1", [P, RINGS[1], 4, D], F32, last)
            S1 = sb("S1", [P, 2, 4, P], F32, last)
            typ_rows = sb("typ_rows", [3 * R, TYPE_RING, GE], I32, last)
            TT = sb("TT", [3 * R, 2, 4, P], BF16, last)
            q = sb("q", [P, 2, D], F32, last)
            x2in = q
            qT = sb("qT", [P, KD, TOK], F32, last)
            qh = sb("qh", [P, 2, KF, TOK], F32, last)
            gw = sb("gw", [P, KD, NE], F32, last)
            gbb = sb("gbb", [P, NE], F32, last)
            b1e = sb("b1e", [P, NE, KF], F32, last)
            b2e = sb("b2e", [NE, D], F32, last)
            logits = sb("logits", [P, 2, NE], F32, last)
            gs = sb("gs", [P, 6, 2, NE], F32, last)
            gcol = sb("gcol", [P, 2, 2], F32, last)
            cwS = sb("cwS", [P, 2, NE], F32, last)
            cwT = sb("cwT", [NE, 2, P], F32, last)
            sd = sb("sd", [P, 2], F32, last)
            rs3 = sb("rs3", [P, 2], F32, last)
            mv3 = sb("mv3", [P, 2, 2], F32, last)
            o = sb("o", [P, 2, D], F32, last)

        bank = [ctx.enter_context(nc.psum_tensor(f"bank{i}", [P, 512], F32)) for i in range(8)]

        s = {n: sem(n) for n in (
            "consts consts2 edges_in edges_ready turns_ready range_ready range_out range_in x_in table0_stats table0_rstd "
            "table0_normed table0_out "
            "update_in gate_in agg_copied aggT_ps aggT_sb agg_ps x1_var x1_sd inv_ready invT_ps invT_sb "
            "hsum_ready mean_ps mean_sb logit_ps soft_in soft_exp chosen_ready row_ready row_ps row_sb "
            "middle_in chosen_in chosen_scaled h0_ready h0T_ps h0T_sb f1_ps f1_sb f2_ps ln1_var ln1_rstd x2_ready "
            "x2_out ln2_var ln2_rstd hn_ready hnT_ps hnT_sb y_ps y_sb root_ps root_sb "
            "experts_in last_in x2_in x3_var x3_sd q_ready qT_ps qT_sb lg_ps exp_in exp_out "
            "cw_ready cwT_ps cwT_sb bias_ps u1_ps u1_sb u2_ps u2_sb o_ready o_out "
            "pool_passed dve_passed").split()}
        y_out = [sem(f"y_out{r}") for r in range(4)]
        rows_in = [sem(f"rows_in{k}") for k in range(TYPE_RING)]
        gathered = [[sem(f"gathered{layer}_{k}") for k in range(RINGS[layer])] for layer in range(2)]
        seg = [{n: sem(f"{n}{layer}") for n in "idx scaled S mm added Sx mmx W Wx TT".split()} for layer in range(2)]

        def turn_ranges(eng, regs, i):
            eng.load(regs, tile_range[0:1, bass.ds(i * len(regs), len(regs))])
            tiles = [eng.snap(r, min_val=0, max_val=NT - 1) for r in regs]
            return list(zip(tiles[0::2], tiles[1::2]))

        def pool_gather(pool, layer):
            G, table, ring, sg = (G0, G1)[layer], (table0, table1)[layer], RINGS[layer], seg[layer]
            with pool.Fori(0, NG // ring) as i:
                for k in range(ring):
                    pool.wait_ge(sg["added"], i * ring + (k + 1)).then_inc(s["pool_passed"], 1)
                    pool.wait_ge(sg["idx"], i * ring + (k + 1)).then_inc(s["pool_passed"], 1)
                    for j in range(4):
                        pool.indirect_dma_start(
                            G[:, k, j, 0:D], None, table[:, :],
                            bass.IndirectOffsetOnAxis(ap=idx_slot[:, k, j:j + 1], axis=0),
                        ).then_inc(gathered[layer][k], 16)

        def act_first_rows(layer):
            for k in range(RINGS[layer]):
                nc.scalar.copy(idx_slot[:, k, :], (src_i, idx1)[layer][:, 4 * k:4 * k + 4]).then_inc(seg[layer]["idx"], 1)

        def act_turn(act, layer, i, units={}):
            idx, ring, sg = (src_i, idx1)[layer], RINGS[layer], seg[layer]
            for k in range(ring):
                g = i * ring + k
                run(units, k)
                act.wait_ge(gathered[layer][k], i * 64 + 64)
                nc.scalar.copy(idx_slot[:, k, :], idx[:, bass.ds((g + ring) * 4, 4)]).then_inc(sg["idx"], 1)
                if layer == 0:
                    for j in range(4):
                        last = nc.scalar.activation(G0[:, k, j, 0:D], G0[:, k, j, 0:D], ACT.Copy,
                                                    scale=w_e[:, bass.ds(g * 4 + j, 1)])
                    last.then_inc(sg["scaled"], 1)

        def run(units, k):
            for unit in units.get(k, ()):
                unit()

        def dve_turn(dve, layer, i, units={}):
            S, ring, sg = (S0, S1)[layer], RINGS[layer], seg[layer]
            width = (GW, D)[layer]

            def one_hot(g, t, slot, inverse_counts, ps):
                dve.drain()
                nc.vector.tensor_scalar(rel_node[:, :], dst_f[:, bass.ds(g * 4, 4)], tile_base[:, bass.ds(t, 1)],
                                        None, ALU.subtract)
                dve.drain()
                if layer == 0:
                    return nc.vector.tensor_tensor(
                        S[:, slot, :, :], iota[:, :].unsqueeze(1).to_broadcast([P, 4, P]),
                        rel_node[:, :].unsqueeze(2).to_broadcast([P, 4, P]), ALU.is_equal)
                inverse_counts()
                for j in range(4):
                    last = nc.vector.scalar_tensor_tensor(
                        out=S[:, slot, j, :], in0=iota[:, :], scalar=rel_node[:, j:j + 1],
                        in1=ps[:, j * P:(j + 1) * P], op0=ALU.is_equal, op1=ALU.mult)
                return last

            def types(k):
                if layer == 0:
                    return nc.vector.tensor_tensor(
                        G0[:, k, :, D:GW], iota8[:, :].unsqueeze(1).to_broadcast([P, 4, R]),
                        typ_f[:, bass.ds((i * ring + k) * 4, 4)].unsqueeze(2).to_broadcast([P, 4, R]), ALU.is_equal)
                dve.wait_ge(rows_in[k % TYPE_RING], i * (16 * (ring // TYPE_RING)) + 16 * (k // TYPE_RING + 1))
                return nc.vector.tensor_scalar(TT[:, k % 2, :, :].rearrange("p j e -> p (j e)"),
                                               typ_rows[:, k % TYPE_RING, :], lane8[0:3 * R, :], None,
                                               ALU.is_equal).then_inc(sg["TT"], 1)

            def add(ps, t):
                rows = acc[:, bass.ds(t, 1), 0:width].rearrange("p a d -> p (a d)")
                return nc.vector.tensor_tensor(rows, rows, ps[:, 0:width], ALU.add)

            ranges = turn_ranges(dve, range_regs_dve, i)
            types(0)
            types(1)
            run(units, -1)
            for k in range(ring + 1):
                if k < ring:
                    g = i * ring + k
                    lo, hi = ranges[k]
                    if 1 <= k < ring - 1:
                        types(k + 1)
                    one_hot(g, lo, k % 2, lambda: dve.wait_ge(sg["W"], i * ring + (k + 1)),
                            bank[2 + k % 2]).then_inc(sg["S"], 1)
                run(units, k)
                if k >= 1:
                    dve.drain()
                    dve.wait_ge(sg["mm"], i * ring + k)
                    add(bank[(k - 1) % 2], ranges[k - 1][0]).then_inc(sg["added"], 1)
                if k < ring:
                    with dve.If(hi > lo):
                        with dve.Fori(lo + 1, hi + 1) as t:
                            dve.reg_add(extra_dve, extra_dve, 1)
                            n = dve.snap(extra_dve, min_val=1, max_val=NG * NT)
                            dve.wait_ge(sg["mm"], g + 1).then_inc(s["dve_passed"], 1)
                            one_hot(g, t, k % 2, lambda: dve.wait_ge(sg["Wx"], n), bank[2 + k % 2]
                                    ).then_inc(sg["Sx"], 1)
                            dve.drain()
                            dve.wait_ge(sg["mmx"], n)
                            add(bank[(k + 1) % 2], t)
                            dve.drain()

        def pe_turn(pe, layer, i, units={}):
            G, S, ring, sg = (G0, G1)[layer], (S0, S1)[layer], RINGS[layer], seg[layer]
            width = (GW, D)[layer]

            def inverse_counts(ps, t, slot):
                for j in range(4):
                    last = pe.matmul(ps[:, j * P:(j + 1) * P], TT[:, slot, j, :],
                                     invT[:, bass.ds(t * P, P)], start=True, stop=True)
                return last

            def product(ps, slot, k):
                for j in range(4):
                    last = pe.matmul(ps[:, 0:width], S[:, slot, j, :], G[:, k, j, 0:width],
                                     start=(j == 0), stop=(j == 3))
                return last

            ranges = turn_ranges(pe, range_regs_pe, i)
            run(units, -1)
            for k in range(-1, ring):
                if k + 1 < ring and layer == 1:
                    pe.wait_ge(sg["TT"], i * ring + (k + 2 + TYPE_RING))
                    inverse_counts(bank[2 + (k + 1) % 2], ranges[k + 1][0], (k + 1) % 2).then_inc(sg["W"], 1)
                if k < 0:
                    continue
                run(units, k)
                g = i * ring + k
                lo, hi = ranges[k]
                if layer == 1:
                    pe.wait_ge(gathered[1][k], i * 64 + 64)
                else:
                    pe.wait_ge(sg["scaled"], g + 1)
                pe.wait_ge(sg["S"], g + 1)
                pe.wait_ge(sg["added"], g + (ring - 1))
                product(bank[k % 2], k % 2, k).then_inc(sg["mm"], 1)
                with pe.If(hi > lo):
                    with pe.Fori(lo + 1, hi + 1) as t:
                        pe.reg_add(extra_pe, extra_pe, 1)
                        n = pe.snap(extra_pe, min_val=1, max_val=NG * NT)
                        if layer == 1:
                            inverse_counts(bank[2 + k % 2], t, k % 2).then_inc(sg["Wx"], 1)
                        pe.wait_ge(sg["Sx"], n)
                        product(bank[(k + 1) % 2], k % 2, k).then_inc(sg["mmx"], 1)

        def turns_of_step(eng, b, turn, early=None, late=None):
            done = eng.value_load(turns[0:1, bass.ds(b, 1)], min_val=0, max_val=TURNS)
            need = eng.value_load(turns[0:1, bass.ds(b + 1, 1)], min_val=0, max_val=TURNS)
            if early is None:
                with eng.If(need > done):
                    with eng.Fori(done, need) as i:
                        turn(i, {})
                return
            for n, units in enumerate((early, late)):
                with eng.If(need > done + n):
                    turn(eng.value_load(turns[0:1, bass.ds(b, 1)], min_val=0, max_val=TURNS - 1 - n) + n, units)
                with eng.If(done + (n + 1) > need):
                    alone(units)
            with eng.If(need > done + 2):
                with eng.Fori(done + 2, need) as i:
                    turn(i, {})

        def alone(units):
            for k in units:
                run(units, k)

        def steps(eng, step):
            step(0, experts=False)
            with eng.Fori(1, NB) as b:
                step(b)
            step(NB, sums=False)

        extra_dve = nc.vector.alloc_register("extra_dve")
        extra_pe = nc.tensor.alloc_register("extra_pe")
        range_regs_dve = [nc.vector.alloc_register(f"range_dve{n}") for n in range(2 * RINGS[0])]
        range_regs_pe = [nc.tensor.alloc_register(f"range_pe{n}") for n in range(2 * RINGS[0])]

        block = ctx.enter_context(nc.Block())

        @block.gpsimd
        def _(pool):
            g = nc.gpsimd
            g.memset(ident[:, :], 0.0).then_inc(s["consts"], 1)
            g.memset(ones[:, :], 1.0).then_inc(s["consts"], 1)
            g.memset(minus_half[:, :], -0.5).then_inc(s["consts"], 1)
            for t, step, num, base, lanes in ((iota, 1, P, 0, 0), (iota8, 1, R, 0, 0), (iota_rev, -1, R, R, 0),
                                              (tile_base, P, NT, 0, 0), (lane_i, 0, 1, 0, 1),
                                              (turn1, 1, TURNS, 1, 0), (bound, 2, NB, 1, 0)):
                g.iota(t[:, :], pattern=[[step, num]], base=base, channel_multiplier=lanes,
                       allow_small_or_imprecise_dtypes=True).then_inc(s["consts"], 1)
            pool.wait_ge(s["consts"], 10)
            g.affine_select(out=ident[:, :], in_=ident[:, :], compare_op=ALU.not_equal, fill=1.0, base=0,
                            pattern=[[-1, P]], channel_multiplier=1).then_inc(s["consts"], 1)
            pool.wait_ge(s["table0_stats"], 1)
            g.tensor_tensor(rstd[:, :], var_eps[:, :], minus_half[:, :], ALU.pow).then_inc(s["table0_rstd"], 1)
            pool.wait_ge(s["table0_out"], 16)
            pool_gather(pool, 0)
            with pool.Fori(0, NB) as b:
                for n, var, out_sem in ((0, s["ln1_var"], s["ln1_rstd"]), (1, s["ln2_var"], s["ln2_rstd"])):
                    pool.wait_ge(var, b + 1)
                    g.tensor_tensor(ln_rs[:, n, :], ln_ve[:, n, :], minus_half[:, 0:2], ALU.pow).then_inc(out_sem, 1)
            for r in range(4):
                pool.wait_ge(y_out[r], 16 * (NT + 1))
            pool_gather(pool, 1)

        @block.sync
        def _(sp):
            for r in range(4):
                sp.sem_inc(y_out[r], 16)
            sp.sem_inc(s["o_out"], 16)
            sp.dma_start(dst_rows[:, :, :], dst_flat.rearrange("(a r c) -> r a c", a=4, c=GE)).then_inc(s["range_in"], 16)
            sp.dma_start(X, tiles_of(x)).then_inc(s["x_in"], 16)
            sp.dma_start(src_i[:, :], src).then_inc(s["edges_in"], 16)
            sp.dma_start(dst_i, dst).then_inc(s["edges_in"], 16)
            sp.dma_start(typ_i, typ).then_inc(s["edges_in"], 16)
            sp.dma_start(w_e[:, :], wgt).then_inc(s["edges_in"], 16)
            sp.dma_start(Wg[:, :, :], W_gnn0.rearrange("(k p) n -> p k n", p=P)).then_inc(s["update_in"], 16)
            sp.wait_ge(s["range_ready"], 1)
            sp.dma_start(range_dram.rearrange("(a r) c -> r a c", a=4), range_i[:, :, :]).then_inc(s["range_out"], 16)
            sp.wait_ge(s["range_out"], 16)
            sp.dma_start(tile_range[:, :], range_dram.rearrange("(a g) c -> a (g c)", a=1)).then_inc(s["range_in"], 16)
            sp.wait_ge(s["table0_normed"], 1)
            sp.dma_start(tiles_of(table0), acc[:, :, 0:D]).then_inc(s["table0_out"], 16)
            sp.wait_ge(seg[0]["added"], NG + RINGS[0])
            sp.wait_ge(s["agg_ps"], NB)
            sp.dma_start(Wr_sb[:, :, :], Wr.rearrange("(k p) n -> p k n", p=P)).then_inc(s["gate_in"], 16)
            sp.dma_start(br_sb[:, :], br.rearrange("(a n) -> a n", a=1)).then_inc(s["gate_in"], 16)
            sp.wait_ge(s["chosen_ready"], 1)
            for n in range(2):
                e = sp.value_load(chosen[0:1, n:n + 1], min_val=0, max_val=NE - 1)
                sp.dma_start(Wsel1[:, n, :, :], W1_0[bass.ds(e, 1), :, :].rearrange("a (k p) f -> p (a k) f", p=P)
                             ).then_inc(s["chosen_in"], 16)
                sp.dma_start(Wsel2[:, n, :, :], W2_0[bass.ds(e, 1), :, :].rearrange("a (k p) d -> p (a k) d", p=P)
                             ).then_inc(s["chosen_in"], 16)
                sp.dma_start(b1s[:, n, :], b1_0[bass.ds(e, 1), :, :].rearrange("a p k -> p (a k)")
                             ).then_inc(s["chosen_in"], 16)
                sp.dma_start(b2s[:, n, :], b2_0[bass.ds(e, 1), :]).then_inc(s["chosen_in"], 16)
            for t, v in ((gam, gamma), (bet, beta), (bias_b, bias1)):
                sp.dma_start(t[:, :], v.rearrange("(a n) -> a n", a=1).to_broadcast([P, D])).then_inc(s["middle_in"], 16)
            for r in range(R):
                sp.dma_start(Wrel[:, :, r * D:(r + 1) * D], W_rel[r].rearrange("(k p) n -> p k n", p=P)
                             ).then_inc(s["middle_in"], 16)
            sp.dma_start(Wrel[:, :, R * D:], W_root.rearrange("(k p) n -> p k n", p=P)).then_inc(s["middle_in"], 16)
            def store_table(b):
                for t in range(2):
                    for r in range(4):
                        sp.wait_ge(s["y_sb"], b * 8 + (4 * t + r + 3))
                        sp.dma_start(table1.rearrange("(t p r) d -> p t (r d)", p=P, r=R)
                                     [:, bass.ds(b * 2 + t, 1), r * 2 * D:(r + 1) * 2 * D].rearrange("p a d -> p (a d)"),
                                     Y[:, r, :]).then_inc(y_out[r], 16)

            def store_x2(b):
                sp.wait_ge(s["x2_ready"], b + 1)
                sp.dma_start(tiles_of(x2_dram)[:, bass.ds(b * 2, 2), :], X[:, bass.ds(b * 2, 2), :]).then_inc(s["x2_out"], 16)

            store_x2(0)
            with sp.Fori(1, NB) as b:
                store_table(b - 1)
                store_x2(b)
            store_table(NB - 1)
            sp.wait_ge(s["x2_out"], 16 * NB)
            sp.wait_ge(s["root_sb"], NT + 2)
            for e in range(NE):
                sp.dma_start(W1e[:, e, :, :], W1_1[e].rearrange("(k p) f -> p k f", p=P)).then_inc(s["experts_in"], 16)
                sp.dma_start(W2e[:, e, :, :], W2_1[e].rearrange("(k p) d -> p k d", p=P)).then_inc(s["experts_in"], 16)
            for r in range(4):
                sp.wait_ge(y_out[r], 16 * (NT + 1))
            sp.dma_start(gw[:, :, :], gate_w.rearrange("(k p) n -> p k n", p=P)).then_inc(s["last_in"], 16)
            sp.dma_start(gbb[:, :], gate_b.rearrange("(a n) -> a n", a=1).to_broadcast([P, NE])).then_inc(s["last_in"], 16)
            sp.dma_start(b1e[:, :, :], b1_1.rearrange("e p k -> p e k")).then_inc(s["last_in"], 16)
            sp.dma_start(b2e[:, :], b2_1).then_inc(s["last_in"], 16)

            def turn(i, units):
                for k in range(RINGS[1]):
                    g = i * RINGS[1] + k
                    sp.wait_ge(seg[1]["TT"], g + 1)
                    sp.dma_start(typ_rows[:, k % TYPE_RING, :], typ_flat.rearrange("(a g) -> a g", a=1)
                                 [:, bass.ds(g * GE, GE)].to_broadcast([3 * R, GE])).then_inc(rows_in[k % TYPE_RING], 16)

            def load_x2(b):
                sp.wait_ge(s["qT_ps"], b + 1)
                sp.dma_start(x2in[:, :, :], tiles_of(x2_dram)[:, bass.ds(b * 2, 2), :]).then_inc(s["x2_in"], 16)

            with sp.Fori(0, NB) as b:
                turns_of_step(sp, b, turn)
                load_x2(b)
            sp.wait_ge(s["o_out"], 16 * (NB + 1))

        @block.scalar
        def _(act):
            act.wait_ge(s["edges_in"], 64)
            act_first_rows(0)
            act.wait_ge(s["turns_ready"], 1)
            with act.Fori(0, NB) as b:
                turns_of_step(act, b, lambda i, units: act_turn(act, 0, i))
                act.wait_ge(s["aggT_ps"], b + 1)
                nc.scalar.copy(aggT[:, :, :, :].rearrange("p k t c -> p (k t c)"), bank[4][:, :]).then_inc(s["aggT_sb"], 1)
                act.wait_ge(s["x1_var"], b + 1)
                nc.scalar.activation(var_sd[:, :], var_sd[:, :], ACT.Sqrt).then_inc(s["x1_sd"], 1)
            for c in range(7):
                act.wait_ge(s["invT_ps"], c + 1)
                n = min(8, NT - 8 * c)
                nc.scalar.copy(invT[:, 8 * c * P:(8 * c + n) * P], bank[4 + c % 2][0:3 * R, :].bitcast(BF16)[:, 0:n * P]
                               ).then_inc(s["invT_sb"], 1)
            for n in range(3):
                act.wait_ge(s["soft_in"], n + 1)
                w = NE if n < 2 else 1
                nc.scalar.activation(gt[:, 1, 0:w], gt[:, 0, 0:w], ACT.Exp).then_inc(s["soft_exp"], 1)
            act.wait_ge(s["row_sb"], 1)
            act.wait_ge(s["chosen_in"], 16 * 8)
            for n in range(2):
                nc.scalar.activation(Wsel2[:, n, :, :], Wsel2[:, n, :, :], ACT.Copy, scale=gate_b0[:, n:n + 1]
                                     ).then_inc(s["chosen_scaled"], 1)

            def experts_part(b):
                act.wait_ge(s["h0T_ps"], b + 1)
                nc.scalar.copy(h0T[:, :, :].rearrange("p k t -> p (k t)"), bank[0][:, :]).then_inc(s["h0T_sb"], 1)
                for u in range(4):
                    act.wait_ge(s["f1_ps"], b * 4 + (u + 1))
                    for v in range(2):
                        n, f = divmod(2 * u + v, KF)
                        gelu = nc.scalar.activation(hT[:, n, f, :], bank[1 + u % 2][:, v * TOK:(v + 1) * TOK],
                                                    ACT.Gelu, bias=b1s[:, n, f:f + 1])
                    gelu.then_inc(s["f1_sb"], 1)

            def table_part(b):
                act.wait_ge(s["hnT_ps"], b + 1)
                nc.scalar.copy(hnT[:, :, :].rearrange("p k t -> p (k t)"), bank[0][:, :]).then_inc(s["hnT_sb"], 1)
                for t in range(2):
                    for r in range(4):
                        act.wait_ge(y_out[r], b * 32 + (16 * t + 16))
                        act.wait_ge(s["y_ps"], b * 8 + (4 * t + r + 1))
                        nc.scalar.copy(Y[:, r, :], bank[4 + r % 2][:, :]).then_inc(s["y_sb"], 1)

            experts_part(0)
            with act.Fori(1, NB) as b:
                experts_part(b)
                table_part(b - 1)
            table_part(NB - 1)
            act_first_rows(1)
            act.wait_ge(s["last_in"], 64)

            def hidden(b, e):
                for u in range(2):
                    act.wait_ge(s["u1_ps"], b * (2 * NE) + (2 * e + u + 1))
                    for v in range(2):
                        f = 2 * u + v
                        gelu = nc.scalar.activation(qh[:, e % 2, f, :], bank[4 + u][:, v * TOK:(v + 1) * TOK],
                                                    ACT.Gelu, bias=b1e[:, e, f:f + 1])
                    gelu.then_inc(s["u1_sb"], 1)

            def spread(b):
                act.wait_ge(s["x3_var"], b + 1)
                nc.scalar.activation(sd[:, :], sd[:, :], ACT.Sqrt).then_inc(s["x3_sd"], 1)

            def transposed(b):
                act.wait_ge(s["qT_ps"], b + 2)
                nc.scalar.copy(qT[:, :, :].rearrange("p k t -> p (k t)"), bank[7][:, :]).then_inc(s["qT_sb"], 1)

            def exps(b):
                act.wait_ge(s["exp_in"], b + 1)
                nc.scalar.activation(gs[:, 1, :, :], gs[:, 0, :, :], ACT.Exp).then_inc(s["exp_out"], 1)

            def store(b):
                act.wait_ge(s["o_ready"], b + 1)
                act.dma_start(tiles_of(out)[:, bass.ds(b * 2, 2), :], o[:, :, :]).then_inc(s["o_out"], 16)

            def step(b, sums=True, experts=True):
                def h(e):
                    return lambda: hidden(b - 1, e)

                early = {0: [lambda: exps(b - 1), h(0), h(1)], 2: [h(2)], 5: [h(3)], 7: [h(4)]}
                late = {0: [h(5)], 3: [h(6)]}
                if not experts:
                    turns_of_step(act, b, lambda i, units: act_turn(act, 1, i))
                elif sums:
                    turns_of_step(act, b, lambda i, units: act_turn(act, 1, i, units), early, late)
                else:
                    alone(early)
                    alone(late)
                if experts:
                    hidden(b - 1, NE - 1)
                if sums:
                    spread(b)
                    transposed(b)
                if experts:
                    store(b - 1)

            steps(act, step)

        @block.tensor
        def _(pe):
            pe.sem_inc(s["qT_ps"], 1)
            pe.wait_ge(s["consts2"], 1)
            pe.wait_ge(s["range_in"], 32)
            pe.reg_mov(extra_pe, 0)
            pe.wait_ge(s["turns_ready"], 1)
            pe.wait_ge(s["update_in"], 16)

            def transposes(ps, tiles, count):
                for t in range(2):
                    for k in range(KD):
                        last = pe.transpose(ps[:, (2 * k + t) * P:(2 * k + t + 1) * P], tiles[:, t, k * P:(k + 1) * P],
                                            ident[:, :])
                return last.then_inc(count, 1)

            with pe.Fori(0, NB) as b:
                turns_of_step(pe, b, lambda i, units: pe_turn(pe, 0, i))
                pe.wait_ge(s["agg_copied"], b + 1)
                transposes(bank[4], aggS, s["aggT_ps"])
                pe.wait_ge(s["aggT_sb"], b + 1)
                for t in range(2):
                    for k in range(KD):
                        mm = pe.matmul(bank[5][:, t * D:(t + 1) * D], aggT[:, k, t, :], Wg[:, k, :],
                                       start=(k == 0), stop=(k == KD - 1))
                mm.then_inc(s["agg_ps"], 1)
            pe.wait_ge(s["gate_in"], 32)
            pe.wait_ge(s["inv_ready"], 1)
            for c in range(7):
                if c >= 2:
                    pe.wait_ge(s["invT_sb"], c - 1)
                for t in range(8 * c, min(8 * c + 8, NT)):
                    tr = pe.transpose(bank[4 + c % 2][0:3 * R, :].bitcast(BF16)[:, (t % 8) * P:(t % 8 + 1) * P],
                                      inv3[:, t, :, :].rearrange("p a r -> p (a r)"), identb[:, :])
                tr.then_inc(s["invT_ps"], 1)
            pe.wait_ge(s["hsum_ready"], 1)
            for k in range(KD):
                mm = pe.matmul(bank[6][:, k:k + 1], hsum[:, k * P:(k + 1) * P], ones[:, 0:1], start=True, stop=True)
            mm.then_inc(s["mean_ps"], 1)
            pe.wait_ge(s["mean_sb"], 1)
            for k in range(KD):
                mm = pe.matmul(bank[7][0:1, 0:NE], mean_sb[:, k:k + 1], Wr_sb[:, k, :], start=(k == 0), stop=(k == KD - 1))
            mm.then_inc(s["logit_ps"], 1)
            pe.wait_ge(s["row_ready"], 1)
            pe.matmul(bank[6][:, 0:2 + D], ones[0:1, :], row[0:1, :], start=True, stop=True).then_inc(s["row_ps"], 1)
            pe.wait_ge(s["chosen_in"], 16 * 8)
            pe.wait_ge(s["middle_in"], 16 * (R + 4))
            pe.wait_ge(s["chosen_scaled"], 2)

            def first_products(b):
                pe.wait_ge(s["h0_ready"], b + 1)
                transposes(bank[0], h0, s["h0T_ps"])
                pe.wait_ge(s["h0T_sb"], b + 1)
                for u in range(4):
                    if u >= 2:
                        pe.wait_ge(s["f1_sb"], b * 4 + (u - 1))
                    for v in range(2):
                        n, f = divmod(2 * u + v, KF)
                        for k in range(KD):
                            mm = pe.matmul(bank[1 + u % 2][:, v * TOK:(v + 1) * TOK],
                                           Wsel1[:, n, k, f * P:(f + 1) * P], h0T[:, k, :],
                                           start=(k == 0), stop=(k == KD - 1))
                    mm.then_inc(s["f1_ps"], 1)

            def second_products(b):
                pe.wait_ge(s["f1_sb"], b * 4 + 4)
                for t in range(2):
                    for n in range(2):
                        for f in range(KF):
                            mm = pe.matmul(bank[3][:, t * D:(t + 1) * D], hT[:, n, f, t * P:(t + 1) * P],
                                           Wsel2[:, n, f, :], start=(n == 0 and f == 0), stop=(n == 1 and f == KF - 1))
                mm.then_inc(s["f2_ps"], 1)

            def transpose_hn(b):
                pe.wait_ge(s["hn_ready"], b + 1)
                transposes(bank[0], hn, s["hnT_ps"])

            def table_products(b):
                pe.wait_ge(s["hnT_sb"], b + 1)
                for t in range(2):
                    for r in range(4):
                        pe.wait_ge(s["y_sb"], b * 8 + (4 * t + r + 1))
                        for k in range(KD):
                            mm = pe.matmul(bank[4 + r % 2][:, :], hnT[:, k, t * P:(t + 1) * P],
                                           Wrel[:, k, r * 2 * D:(r + 1) * 2 * D], start=(k == 0), stop=(k == KD - 1))
                        mm.then_inc(s["y_ps"], 1)
                    pe.wait_ge(s["root_sb"], b * 2 + (t + 1))
                    for k in range(KD):
                        mm = pe.matmul(bank[6 + t][:, 0:D], hnT[:, k, t * P:(t + 1) * P], Wrel[:, k, R * D:],
                                       start=(k == 0), stop=(k == KD - 1))
                    mm.then_inc(s["root_ps"], 1)

            first_products(0)
            second_products(0)
            with pe.Fori(1, NB) as b:
                first_products(b)
                transpose_hn(b - 1)
                second_products(b)
                table_products(b - 1)
            transpose_hn(NB - 1)
            table_products(NB - 1)
            pe.reg_mov(extra_pe, 0)
            pe.wait_ge(s["last_in"], 64)
            pe.wait_ge(s["experts_in"], 16 * 2 * NE)

            def hidden(b, e):
                for u in range(2):
                    pe.wait_ge(s["u1_sb"], b * (2 * NE) + (2 * e + u + 1))
                    for v in range(2):
                        f = 2 * u + v
                        for k in range(KD):
                            mm = pe.matmul(bank[4 + u][:, v * TOK:(v + 1) * TOK], W1e[:, e, k, f * P:(f + 1) * P],
                                           qT[:, k, :], start=(k == 0), stop=(k == KD - 1))
                    mm.then_inc(s["u1_ps"], 1)

            def output(b, e):
                pe.wait_ge(s["u1_sb"], b * (2 * NE) + (2 * e + 4))
                pe.wait_ge(s["u2_sb"], b * NE + (e + 1))
                for t in range(2):
                    for f in range(KF):
                        mm = pe.matmul(bank[6][:, t * D:(t + 1) * D], qh[:, e % 2, f, t * P:(t + 1) * P],
                                       W2e[:, e, f, :], start=(f == 0), stop=(f == KF - 1))
                mm.then_inc(s["u2_ps"], 1)

            def transpose_gates(b):
                pe.wait_ge(s["cw_ready"], b + 1)
                for t in range(2):
                    tr = pe.transpose(bank[7][0:NE, t * P:(t + 1) * P], cwS[:, t, :], ident[:, :])
                tr.then_inc(s["cwT_ps"], 1)

            def gated_biases(b):
                pe.wait_ge(s["cwT_sb"], b + 1)
                for t in range(2):
                    mm = pe.matmul(bank[7][:, t * D:(t + 1) * D], cwT[:, t, :], b2e[:, :], start=True, stop=True)
                mm.then_inc(s["bias_ps"], 1)

            def transpose_q(b):
                pe.wait_ge(s["q_ready"], b + 1)
                transposes(bank[7], q, s["qT_ps"])

            def logit_products(b):
                pe.wait_ge(s["qT_sb"], b + 1)
                for t in range(2):
                    for k in range(KD):
                        mm = pe.matmul(bank[7][:, t * NE:(t + 1) * NE], qT[:, k, t * P:(t + 1) * P],
                                       gw[:, k, :], start=(k == 0), stop=(k == KD - 1))
                mm.then_inc(s["lg_ps"], 1)

            def step(b, sums=True, experts=True):
                def h(e):
                    return lambda: hidden(b - 1, e)

                def y(e):
                    return lambda: output(b - 1, e)

                early = {-1: [h(0)], 0: [h(1)], 1: [lambda: transpose_gates(b - 1), y(0)],
                         2: [lambda: gated_biases(b - 1), h(2)], 4: [y(1)], 5: [h(3)], 6: [y(2)], 7: [h(4)]}
                late = {-1: [y(3)], 0: [h(5)], 2: [y(4)], 3: [h(6)], 5: [y(5)]}
                if not experts:
                    turns_of_step(pe, b, lambda i, units: pe_turn(pe, 1, i))
                elif sums:
                    turns_of_step(pe, b, lambda i, units: pe_turn(pe, 1, i, units), early, late)
                else:
                    alone(early)
                    alone(late)
                if experts:
                    hidden(b - 1, NE - 1)
                    output(b - 1, NE - 2)
                if sums:
                    transpose_q(b)
                if experts:
                    output(b - 1, NE - 1)
                if sums:
                    logit_products(b)

            steps(pe, step)

        @block.vector
        def _(dve):
            v = nc.vector
            dve.drain().then_inc(s["y_sb"], 2)
            dve.drain().then_inc(s["root_sb"], 2)
            dve.drain().then_inc(s["u1_sb"], 2)
            dve.drain().then_inc(s["u2_sb"], 1)

            def row_stats(rows, b):
                for t in range(2):
                    v.bn_stats(stats[:, t, :], rows[:, bass.ds(b * 2 + t, 1), 0:D].rearrange("p a d -> p (a d)"))
                dve.drain()
                for t in range(2):
                    v.bn_aggr(mv2[:, t, :], stats[:, t, :])
                dve.drain()
                v.tensor_copy(mv[:, bass.ds(b * 2, 2), :], mv2[:, :, :])

            dve.wait_ge(s["consts"], 11)
            v.tensor_copy(identb[:, :], ident[:, :])
            v.tensor_scalar(lane8_i[:, :], lane_i[:, :], R - 1, None, ALU.bitwise_and)
            dve.drain()
            v.tensor_copy(lane8[:, :], lane8_i[:, :]).then_inc(s["consts2"], 1)
            dve.wait_ge(s["range_in"], 16)
            v.tensor_reduce(range_n[:, :, 0:1], dst_rows[:, :, :], AX.X, ALU.min)
            v.tensor_reduce(range_n[:, :, 1:2], dst_rows[:, :, :], AX.X, ALU.max)
            dve.drain()
            v.tensor_scalar(range_i[:, :, :], range_n[:, :, :], 7, None, ALU.arith_shift_right).then_inc(s["range_ready"], 1)
            dve.wait_ge(s["x_in"], 16)
            with dve.Fori(0, NB) as b:
                row_stats(X, b)
            dve.drain()
            v.tensor_scalar(var_eps[:, :], mv[:, :, 1], EPS, None, ALU.add).then_inc(s["table0_stats"], 1)
            dve.wait_ge(s["table0_rstd"], 1)
            with dve.Fori(0, NT) as t:
                v.tensor_scalar(acc[:, bass.ds(t, 1), 0:D].rearrange("p a d -> p (a d)"),
                                X[:, bass.ds(t, 1), :].rearrange("p a d -> p (a d)"),
                                mv[:, bass.ds(t, 1), 0:1].rearrange("p a d -> p (a d)"), rstd[:, bass.ds(t, 1)],
                                ALU.subtract, ALU.mult)
            dve.drain().then_inc(s["table0_normed"], 1)
            dve.wait_ge(s["edges_in"], 64)
            v.tensor_copy(dst_f[:, :], dst_i)
            dve.drain()
            v.tensor_copy(typ_f, typ_i)
            v.memset(idx1[:, NG * 4:], 0)
            v.scalar_tensor_tensor(out=idx1[:, 0:NG * 4], in0=src_i[:, 0:NG * 4], scalar=float(R), in1=typ_i,
                                   op0=ALU.mult, op1=ALU.add)
            dve.wait_ge(s["table0_out"], 16)
            v.memset(acc[:, :, :], 0.0)
            dve.wait_ge(s["range_in"], 32)
            v.tensor_reduce(turn_lo[:, :], tile_range[:, :].rearrange("a (i k c) -> a i c k", k=RINGS[1], c=2)[:, :, 0, :],
                            AX.X, ALU.min)
            dve.drain()
            v.tensor_tensor(turn_of[:, :, :], turn_lo[:, :].unsqueeze(1).to_broadcast([1, NB, TURNS]),
                            bound[:, :].unsqueeze(2).to_broadcast([1, NB, TURNS]), ALU.is_le)
            dve.drain()
            v.tensor_tensor(turn_of[:, :, :], turn_of[:, :, :], turn1[:, :].unsqueeze(1).to_broadcast([1, NB, TURNS]),
                            ALU.mult)
            dve.drain()
            v.tensor_reduce(turns_f[:, :], turn_of[:, :, :], AX.X, ALU.max)
            v.memset(turns[:, 0:1], 0)
            dve.drain()
            v.tensor_copy(turns[:, 1:], turns_f[:, :])
            dve.drain().then_inc(s["turns_ready"], 1)
            v.memset(hsum[:, :], 0.0)
            dve.drain().then_inc(seg[0]["added"], RINGS[0])
            dve.reg_mov(extra_dve, 0)
            with dve.Fori(0, NB) as b:
                turns_of_step(dve, b, lambda i, units: dve_turn(dve, 0, i))
                dve.drain()
                v.tensor_copy(aggS[:, :, :], acc[:, bass.ds(b * 2, 2), 0:D]).then_inc(s["agg_copied"], 1)
                dve.wait_ge(s["agg_ps"], b + 1)
                v.tensor_tensor(X[:, bass.ds(b * 2, 2), :], X[:, bass.ds(b * 2, 2), :],
                                bank[5][:, :].rearrange("p (t d) -> p t d", t=2), ALU.add)
                dve.drain()
                row_stats(X, b)
                v.tensor_scalar(var_sd[:, :], mv2[:, :, 1], EPS, None, ALU.add).then_inc(s["x1_var"], 1)
                dve.wait_ge(s["x1_sd"], b + 1)
                v.reciprocal(rstd[:, bass.ds(b * 2, 2)], var_sd[:, :])
                for t in range(2):
                    dve.drain()
                    v.scalar_tensor_tensor(out=hsum[:, :], in0=X[:, bass.ds(b * 2 + t, 1), :].rearrange("p a d -> p (a d)"),
                                           scalar=rstd[:, bass.ds(b * 2 + t, 1)], in1=hsum[:, :],
                                           op0=ALU.mult, op1=ALU.add)
            dve.drain()
            v.tensor_scalar(inv[:, :, :], acc[:, :, D:GW], 1.0, None, ALU.max)
            dve.drain()
            v.reciprocal(inv[:, :, :], inv[:, :, :])
            for part in range(3):
                dve.drain()
                v.tensor_copy(inv3[:, :, part, :], inv[:, :, :])
                if part < 2:
                    dve.drain()
                    v.tensor_tensor(inv[:, :, :], inv[:, :, :], inv3[:, :, part, :], ALU.subtract)
            dve.drain().then_inc(s["inv_ready"], 1)
            v.tensor_tensor(rm[:, :], rstd[:, :], mv[:, :, 0], ALU.mult)
            dve.drain()
            v.tensor_reduce(rm_sum[:, :], rm[:, :], AX.X, ALU.add)
            dve.drain()
            v.tensor_scalar(hsum[:, :], hsum[:, :], rm_sum[:, :], None, ALU.subtract).then_inc(s["hsum_ready"], 1)
            dve.wait_ge(s["mean_ps"], 1)
            v.tensor_scalar(mean_sb[:, :], bank[6][:, 0:KD], 1.0 / N, None, ALU.mult).then_inc(s["mean_sb"], 1)

            def softmax(src_row, n):
                v.tensor_reduce(gc[:, 0:1], src_row, AX.X, ALU.max)
                dve.drain()
                v.tensor_scalar(gt[:, 0, :], src_row, gc[:, 0:1], None, ALU.subtract).then_inc(s["soft_in"], 1)
                dve.wait_ge(s["soft_exp"], n)
                v.tensor_reduce(gc[:, 1:2], gt[:, 1, :], AX.X, ALU.add)
                dve.drain()
                v.reciprocal(gc[:, 2:3], gc[:, 1:2])
                dve.drain()
                v.tensor_scalar(gt[:, 3, :], gt[:, 1, :], gc[:, 2:3], None, ALU.mult)
                dve.drain()

            dve.wait_ge(s["gate_in"], 32)
            dve.wait_ge(s["logit_ps"], 1)
            v.tensor_tensor(gt[:, 2, :], bank[7][0:1, 0:NE], br_sb[:, :], ALU.add)
            dve.drain()
            softmax(gt[:, 2, :], 1)
            v.tensor_scalar(gt[:, 4, :], gt[:, 3, :], float(N), CAPACITY, ALU.mult, ALU.max)
            dve.drain()
            v.reciprocal(gt[:, 5, :], gt[:, 4, :])
            dve.drain()
            v.scalar_tensor_tensor(out=gt[:, 6, :], in0=gt[:, 5, :], scalar=CAPACITY, in1=gt[:, 3, :],
                                   op0=ALU.mult, op1=ALU.mult)
            dve.drain()
            softmax(gt[:, 6, :], 2)
            v.tensor_copy(gt[:, 4, :], gt[:, 3, :])
            dve.drain()
            for n in range(2):
                v.tensor_reduce(gc[:, 4 + n:5 + n], gt[:, 4, :], AX.X, ALU.max)
                dve.drain()
                v.scalar_tensor_tensor(out=gt[:, 7, :], in0=gt[:, 4, :], scalar=gc[:, 4 + n:5 + n],
                                       in1=iota_rev[0:1, :], op0=ALU.is_equal, op1=ALU.mult)
                dve.drain()
                v.tensor_reduce(gc[:, 6 + n:7 + n], gt[:, 7, :], AX.X, ALU.max)
                dve.drain()
                v.tensor_scalar(gt[:, 8, :], gt[:, 7, :], gc[:, 6 + n:7 + n], None, ALU.is_equal)
                dve.drain()
                v.scalar_tensor_tensor(out=gt[:, 4, :], in0=gt[:, 8, :], scalar=-4.0, in1=gt[:, 4, :],
                                       op0=ALU.mult, op1=ALU.add)
                dve.drain()
            v.tensor_tensor(gt[:, 0, 0:1], gc[:, 5:6], gc[:, 4:5], ALU.subtract).then_inc(s["soft_in"], 1)
            dve.wait_ge(s["soft_exp"], 3)
            v.tensor_scalar(gc[:, 8:9], gt[:, 1, 0:1], 1.0, None, ALU.add)
            dve.drain()
            v.reciprocal(gc[:, 9:10], gc[:, 8:9])
            dve.drain()
            v.tensor_tensor(gc[:, 10:11], gc[:, 9:10], gt[:, 1, 0:1], ALU.mult)
            dve.wait_ge(s["invT_sb"], 7)
            dve.drain()
            v.tensor_copy(gates[:, :], gc[:, 9:11])
            v.tensor_scalar(chosen[:, :], gc[:, 6:8], -1.0, float(NE), ALU.mult, ALU.add).then_inc(s["chosen_ready"], 1)
            dve.wait_ge(s["chosen_in"], 16 * 8)
            dve.drain()
            v.tensor_copy(row[:, 0:2], gates[:, :])
            v.tensor_scalar(row[:, 2:], b2s[:, 0, :], gates[:, 0:1], None, ALU.mult)
            dve.drain()
            v.scalar_tensor_tensor(out=row[:, 2:], in0=b2s[:, 1, :], scalar=gates[:, 1:2], in1=row[:, 2:],
                                   op0=ALU.mult, op1=ALU.add)
            dve.drain().then_inc(s["row_ready"], 1)
            dve.wait_ge(s["row_ps"], 1)
            v.tensor_copy(gate_b0[:, :], bank[6][:, 0:2])
            v.tensor_copy(b2g[:, :], bank[6][:, 2:2 + D])
            dve.drain().then_inc(s["row_sb"], 1)
            dve.wait_ge(s["middle_in"], 16 * (R + 4))

            def per_tile(t):
                return t[:, :].unsqueeze(1).to_broadcast([P, 2, D])

            def make_h0(b):
                for t in range(2):
                    v.tensor_scalar(h0[:, t, :], X[:, bass.ds(b * 2 + t, 1), :].rearrange("p a d -> p (a d)"),
                                    mv[:, bass.ds(b * 2 + t, 1), 0:1].rearrange("p a d -> p (a d)"),
                                    rstd[:, bass.ds(b * 2 + t, 1)], ALU.subtract, ALU.mult)
                dve.drain().then_inc(s["h0_ready"], 1)

            def make_x2(b, go_on=True):
                batch = bass.ds(b * 2, 2)
                dve.wait_ge(s["f2_ps"], b + 1)
                v.tensor_tensor(z[:, :, :], bank[3][:, :].rearrange("p (t d) -> p t d", t=2), h0[:, :, :], ALU.add)
                dve.drain()
                if go_on:
                    make_h0(b + 1)
                v.tensor_tensor(z[:, :, :], z[:, :, :], per_tile(b2g), ALU.add)
                dve.drain()
                for n, tile, var, rs in ((0, z, s["ln1_var"], s["ln1_rstd"]), (1, None, s["ln2_var"], s["ln2_rstd"])):
                    for t in range(2):
                        a = z[:, t, :] if n == 0 else X[:, bass.ds(b * 2 + t, 1), :].rearrange("p a d -> p (a d)")
                        v.bn_stats(stats[:, t, :], a)
                    dve.drain()
                    for t in range(2):
                        v.bn_aggr(ln_mv[:, n, t, :], stats[:, t, :])
                    dve.drain()
                    v.tensor_scalar(ln_ve[:, n, :], ln_mv[:, n, :, 1], EPS, None, ALU.add).then_inc(var, 1)
                    dve.wait_ge(rs, b + 1)
                    for t in range(2):
                        a = z[:, t, :] if n == 0 else X[:, bass.ds(b * 2 + t, 1), :].rearrange("p a d -> p (a d)")
                        v.tensor_scalar((z if n == 0 else hn)[:, t, :], a, ln_mv[:, n, t, 0:1], ln_rs[:, n, t:t + 1],
                                        ALU.subtract, ALU.mult)
                    dve.drain()
                    if n == 0:
                        v.tensor_tensor(z[:, :, :], z[:, :, :], per_tile(gam), ALU.mult)
                        dve.drain()
                        v.tensor_tensor(z[:, :, :], z[:, :, :], per_tile(bet), ALU.add)
                        dve.drain()
                        v.tensor_tensor(X[:, batch, :], X[:, batch, :], z[:, :, :], ALU.add)
                        dve.drain().then_inc(s["x2_ready"], 1)
                dve.drain().then_inc(s["hn_ready"], 1)

            def start_sums(b):
                for t in range(2):
                    dve.wait_ge(s["root_ps"], b * 2 + (t + 1))
                    v.tensor_tensor(acc[:, bass.ds(b * 2 + t, 1), 0:D].rearrange("p a d -> p (a d)"), bank[6 + t][:, 0:D],
                                    bias_b[:, :], ALU.add).then_inc(s["root_sb"], 1)

            make_h0(0)
            make_x2(0)
            with dve.Fori(1, NB - 1) as b:
                make_x2(b)
                start_sums(b - 1)
            make_x2(NB - 1, go_on=False)
            start_sums(NB - 2)
            start_sums(NB - 1)
            for r in range(4):
                dve.wait_ge(y_out[r], 16 * (NT + 1))
            dve.drain().then_inc(seg[1]["added"], RINGS[1])
            dve.drain().then_inc(seg[1]["TT"], TYPE_RING)
            dve.reg_mov(extra_dve, 0)
            dve.wait_ge(s["last_in"], 64)

            def over_experts(col):
                return col.unsqueeze(2).to_broadcast([P, 2, NE])

            rev = iota_rev[:, :].unsqueeze(1).to_broadcast([P, 2, NE])

            def make_gates(b):
                dve.drain()
                dve.wait_ge(s["lg_ps"], b + 1)
                v.tensor_tensor(logits[:, :, :], bank[7][:, 0:2 * NE].rearrange("p (t e) -> p t e", t=2),
                                gbb[:, :].unsqueeze(1).to_broadcast([P, 2, NE]), ALU.add)
                dve.drain()
                v.tensor_reduce(gcol[:, 0, :], logits[:, :, :], AX.X, ALU.max)
                dve.drain()
                v.tensor_tensor(gs[:, 0, :, :], logits[:, :, :], over_experts(gcol[:, 0, :]), ALU.subtract
                                ).then_inc(s["exp_in"], 1)
                dve.wait_ge(s["exp_out"], b + 1)
                v.tensor_reduce(gcol[:, 0, :], gs[:, 1, :, :], AX.X, ALU.add)
                dve.drain()
                v.reciprocal(gcol[:, 1, :], gcol[:, 0, :])
                dve.drain()
                v.tensor_tensor(gs[:, 0, :, :], gs[:, 1, :, :], over_experts(gcol[:, 1, :]), ALU.mult)
                dve.drain()
                v.tensor_copy(gs[:, 1, :, :], gs[:, 0, :, :])
                for n in range(2):
                    dve.drain()
                    v.tensor_reduce(gcol[:, 0, :], gs[:, 1, :, :], AX.X, ALU.max)
                    dve.drain()
                    v.tensor_tensor(gs[:, 2, :, :], gs[:, 1, :, :], over_experts(gcol[:, 0, :]), ALU.is_equal)
                    dve.drain()
                    v.tensor_tensor(gs[:, 2, :, :], gs[:, 2, :, :], rev, ALU.mult)
                    dve.drain()
                    v.tensor_reduce(gcol[:, 1, :], gs[:, 2, :, :], AX.X, ALU.max)
                    dve.drain()
                    v.tensor_tensor(gs[:, 3 + n, :, :], gs[:, 2, :, :], over_experts(gcol[:, 1, :]), ALU.is_equal)
                    dve.drain()
                    v.scalar_tensor_tensor(out=gs[:, 1, :, :], in0=gs[:, 3 + n, :, :], scalar=-4.0, in1=gs[:, 1, :, :],
                                           op0=ALU.mult, op1=ALU.add)
                v.tensor_tensor(gs[:, 3, :, :], gs[:, 3, :, :], gs[:, 4, :, :], ALU.add)
                dve.drain()
                v.tensor_tensor(cwS[:, :, :], gs[:, 3, :, :], gs[:, 0, :, :], ALU.mult).then_inc(s["cw_ready"], 1)

            def norm(b):
                batch = bass.ds(b * 2, 2)
                dve.drain()
                dve.wait_ge(s["x2_in"], b * 16 + 16)
                v.scalar_tensor_tensor(out=acc[:, batch, 0:D], in0=acc[:, batch, 0:D], scalar=0.0, in1=x2in[:, :, :],
                                       op0=ALU.max, op1=ALU.add)
                dve.drain()
                for t in range(2):
                    v.bn_stats(stats[:, t, :], acc[:, bass.ds(b * 2 + t, 1), 0:D].rearrange("p a d -> p (a d)"))
                dve.drain()
                for t in range(2):
                    v.bn_aggr(mv3[:, t, :], stats[:, t, :])
                dve.drain()
                v.tensor_scalar(sd[:, :], mv3[:, :, 1], EPS, None, ALU.add).then_inc(s["x3_var"], 1)
                dve.wait_ge(s["x3_sd"], b + 1)
                v.reciprocal(rs3[:, :], sd[:, :])
                dve.drain()
                for t in range(2):
                    v.tensor_scalar(q[:, t, :], acc[:, bass.ds(b * 2 + t, 1), 0:D].rearrange("p a d -> p (a d)"),
                                    mv3[:, t, 0:1], rs3[:, t:t + 1], ALU.subtract, ALU.mult)
                dve.drain().then_inc(s["q_ready"], 1)

            def gates_copied(b):
                dve.wait_ge(s["cwT_ps"], b + 1)
                v.tensor_copy(cwT[:, :, :], bank[7][0:NE, 0:2 * P].rearrange("p (t c) -> p t c", t=2)
                              ).then_inc(s["cwT_sb"], 1)

            def start_output(b):
                dve.wait_ge(s["bias_ps"], b + 1)
                dve.wait_ge(s["o_out"], b * 16 + 16)
                v.tensor_tensor(o[:, :, :], acc[:, bass.ds(b * 2, 2), 0:D],
                                bank[7][:, :].rearrange("p (t d) -> p t d", t=2), ALU.add)

            def add_expert(b, e):
                dve.drain()
                dve.wait_ge(s["u2_ps"], b * NE + (e + 1))
                for t in range(2):
                    fma = v.scalar_tensor_tensor(out=o[:, t, :], in0=bank[6][:, t * D:(t + 1) * D],
                                                 scalar=cwS[:, t, e:e + 1], in1=o[:, t, :], op0=ALU.mult, op1=ALU.add)
                fma.then_inc(s["u2_sb"], 1)

            def step(b, sums=True, experts=True):
                def y(e):
                    return lambda: add_expert(b - 1, e)

                early = {-1: [lambda: make_gates(b - 1)], 1: [lambda: gates_copied(b - 1)],
                         3: [lambda: start_output(b - 1), y(0)], 5: [y(1)], 7: [y(2)]}
                late = {0: [y(3)], 3: [y(4)], 6: [y(5)]}
                if not experts:
                    turns_of_step(dve, b, lambda i, units: dve_turn(dve, 1, i))
                elif sums:
                    turns_of_step(dve, b, lambda i, units: dve_turn(dve, 1, i, units), early, late)
                else:
                    alone(early)
                    alone(late)
                if sums:
                    norm(b)
                if experts:
                    add_expert(b - 1, NE - 2)
                    add_expert(b - 1, NE - 1)
                    dve.drain().then_inc(s["o_ready"], 1)

            steps(dve, step)


def kernel(**inputs):
    import numpy as _np
    import concourse.bacc as _bacc
    from concourse import mybir as _mybir
    from concourse.bass_utils import run_bass_kernel_spmd as _run

    a = {k: _np.ascontiguousarray(v) for k, v in inputs.items()}
    pad = NG * GE - EDGES

    def padded(v, value, more=0):
        return _np.concatenate([v, _np.full(pad + more, value, v.dtype)])

    def by_partition(v):
        return _np.ascontiguousarray(v.reshape(-1, P).T)

    def hidden_bias(v):
        return _np.ascontiguousarray(v.reshape(NE, KF, P).transpose(0, 2, 1))

    dst_flat = padded(a["dst"], PAD_NODE)
    typ_flat = padded(a["edge_type_8"], 0)
    ins = {
        "x": _np.concatenate([a["x"], _np.zeros((NP - N, D), a["x"].dtype)]),
        "src": by_partition(padded(a["src"], 0, RINGS[0] * GE)),
        "dst": by_partition(dst_flat),
        "typ": by_partition(typ_flat),
        "wgt": by_partition(padded(a["edge_weight"], 0)),
        "dst_flat": dst_flat,
        "typ_flat": typ_flat,
        "W_gnn0": a["L0_gnn_weight"],
        "Wr": a["L0_ffn_Wr"],
        "br": a["L0_ffn_br"],
        "W1_0": a["L0_ffn_W1"],
        "b1_0": hidden_bias(a["L0_ffn_b1"]),
        "W2_0": a["L0_ffn_W2"],
        "b2_0": a["L0_ffn_b2"],
        "gamma": a["L0_ffn_gamma"],
        "beta": a["L0_ffn_beta"],
        "W_rel": a["L1_gnn_W"],
        "W_root": a["L1_gnn_W_root"],
        "bias1": a["L1_gnn_bias"],
        "gate_w": a["L1_ffn_gate_w"],
        "gate_b": a["L1_ffn_gate_b"],
        "W1_1": a["L1_ffn_W1"],
        "b1_1": hidden_bias(a["L1_ffn_b1"]),
        "W2_1": a["L1_ffn_W2"],
        "b2_1": a["L1_ffn_b2"],
    }
    nc = _bacc.Bacc("TRN2", target_bir_lowering=False, num_devices=1)
    arrays, args = {}, []
    for name, v in ins.items():
        arrays[f"in_{name}"] = v
        args.append(nc.dram_tensor(f"in_{name}", v.shape, _mybir.dt.from_np(v.dtype), kind="ExternalInput").ap())
    out = nc.dram_tensor("out_0_dram", (NP, D), _mybir.dt.float32, kind="ExternalOutput").ap()
    gnn_ffn_two_layers(nc, *args, out)
    r = _run(nc, [arrays], core_ids=[0])
    return r.results[0]["out_0_dram"][:N]
```
